# Optimizing a Trainium2 kernel written in Bass

```python
import numpy as np
import jax
import jax.numpy as jnp

def _softmax(x, axis=-1):
    return jax.nn.softmax(x, axis=axis)

def _gelu(x):
    return jax.nn.gelu(x, approximate=True)

def _silu(x):
    return jax.nn.silu(x)

def _sigmoid(x):
    return jax.nn.sigmoid(x)

def _layernorm(x, axis=-1, eps=1e-05):
    m = jnp.mean(x, axis=axis, keepdims=True)
    v = jnp.var(x, axis=axis, keepdims=True)
    return (x - m) / jnp.sqrt(v + eps)

def _scatter_add(tgt, idx, src, axis=0):
    return tgt.at[idx].add(src)

def _segment_sum(src, seg, n):
    return jax.ops.segment_sum(src, seg, n)
kernel_name = 'mk_macaron_d1_jaxref_r8_b29181'

def setup_inputs(seed: int=0):
    np.random.seed(seed)
    _w = jnp.asarray

    def _L0_attn_setup():
        import jax, jax.numpy as jnp
        import numpy as np
        import math
        E = 256
        H = 16
        HKV = 8
        NREP = H // HKV
        HD = E // H // 2
        DEPTH = 12
        LAMBDA_INIT = 0.8 - 0.6 * math.exp(-0.3 * DEPTH)
        EPS = 1e-06

        def _rotary(x, cos, sin):
            d = x.shape[-1] // 2
            x1, x2 = (x[..., :d], x[..., d:])
            c = cos[None, :, None, :]
            si = sin[None, :, None, :]
            return jnp.concatenate([x1 * c + x2 * si, -x1 * si + x2 * c], axis=-1)
        key = jax.random.key(seed)
        ks = jax.random.split(key, 10)
        s = lambda fan_in: 1.0 / np.sqrt(fan_in)
        return {'x': jax.random.normal(ks[0], (2, 256, E), jnp.float32), 'Wq': jax.random.normal(ks[1], (E, E), jnp.float32) * s(E), 'Wk': jax.random.normal(ks[2], (E, E // NREP), jnp.float32) * s(E), 'Wv': jax.random.normal(ks[3], (E, E // NREP), jnp.float32) * s(E), 'Wo': jax.random.normal(ks[4], (E, E), jnp.float32) * s(E), 'lam_q1': jax.random.normal(ks[5], (HD,), jnp.float32) * 0.1, 'lam_k1': jax.random.normal(ks[6], (HD,), jnp.float32) * 0.1, 'lam_q2': jax.random.normal(ks[7], (HD,), jnp.float32) * 0.1, 'lam_k2': jax.random.normal(ks[8], (HD,), jnp.float32) * 0.1, 'g': jnp.ones((2 * HD,), jnp.float32)}
    _L0_attn_in = _L0_attn_setup()

    def _L0_ffn_setup():
        import jax, jax.numpy as jnp
        import numpy as np
        E, H, I = (8, 256, 512)
        TOP_K = 1
        B, S = (1, 256)
        key = jax.random.key(seed)
        ks = jax.random.split(key, 7)
        std = 0.02
        return {'hidden_states': jax.random.normal(ks[0], (B, S, H), dtype=jnp.float32), 'router_w': jax.random.normal(ks[1], (E, H), dtype=jnp.float32) * std, 'gate_up_proj': jax.random.normal(ks[2], (E, H, 2 * I), dtype=jnp.float32) * std, 'down_proj': jax.random.normal(ks[3], (E, I, H), dtype=jnp.float32) * std, 'shared_gate_w': jax.random.normal(ks[4], (H, I), dtype=jnp.float32) * std, 'shared_up_w': jax.random.normal(ks[5], (H, I), dtype=jnp.float32) * std, 'shared_down_w': jax.random.normal(ks[6], (I, H), dtype=jnp.float32) * std}
    _L0_ffn_in = _L0_ffn_setup()
    _d = {'L0_attn_x': _L0_attn_in['x'], 'L0_attn_Wq': _L0_attn_in['Wq'], 'L0_attn_Wk': _L0_attn_in['Wk'], 'L0_attn_Wv': _L0_attn_in['Wv'], 'L0_attn_Wo': _L0_attn_in['Wo'], 'L0_attn_lam_q1': _L0_attn_in['lam_q1'], 'L0_attn_lam_k1': _L0_attn_in['lam_k1'], 'L0_attn_lam_q2': _L0_attn_in['lam_q2'], 'L0_attn_lam_k2': _L0_attn_in['lam_k2'], 'L0_attn_g': _L0_attn_in['g'], 'L0_ffn_router_w': _L0_ffn_in['router_w'], 'L0_ffn_gate_up_proj': _L0_ffn_in['gate_up_proj'], 'L0_ffn_down_proj': _L0_ffn_in['down_proj'], 'L0_ffn_shared_gate_w': _L0_ffn_in['shared_gate_w'], 'L0_ffn_shared_up_w': _L0_ffn_in['shared_up_w'], 'L0_ffn_shared_down_w': _L0_ffn_in['shared_down_w']}
    _x0 = _d['L0_attn_x']
    _d['L0_attn_x'] = jax.random.normal(jax.random.fold_in(jax.random.key(seed), 1), (4, 256, 256), dtype=_x0.dtype)
    del _x0
    return _d

def reference(L0_attn_x, L0_attn_Wq, L0_attn_Wk, L0_attn_Wv, L0_attn_Wo, L0_attn_lam_q1, L0_attn_lam_k1, L0_attn_lam_q2, L0_attn_lam_k2, L0_attn_g, L0_ffn_router_w, L0_ffn_gate_up_proj, L0_ffn_down_proj, L0_ffn_shared_gate_w, L0_ffn_shared_up_w, L0_ffn_shared_down_w):

    def _L0_attn_ref(x, Wq, Wk, Wv, Wo, lam_q1, lam_k1, lam_q2, lam_k2, g):
        import jax, jax.numpy as jnp
        import numpy as np
        import math
        E = 256
        H = 16
        HKV = 8
        NREP = H // HKV
        HD = E // H // 2
        DEPTH = 12
        LAMBDA_INIT = 0.8 - 0.6 * math.exp(-0.3 * DEPTH)
        EPS = 1e-06

        def _rotary(x, cos, sin):
            d = x.shape[-1] // 2
            x1, x2 = (x[..., :d], x[..., d:])
            c = cos[None, :, None, :]
            si = sin[None, :, None, :]
            return jnp.concatenate([x1 * c + x2 * si, -x1 * si + x2 * c], axis=-1)
        B, T, _ = x.shape
        q = (x @ Wq).reshape(B, T, 2 * H, HD)
        k = (x @ Wk).reshape(B, T, 2 * HKV, HD)
        v = (x @ Wv).reshape(B, T, HKV, 2 * HD)
        inv_freq = 1.0 / 10000.0 ** (jnp.arange(0, HD, 2, dtype=jnp.float32) / HD)
        freqs = jnp.arange(T, dtype=jnp.float32)[:, None] * inv_freq[None, :]
        cos, sin = (jnp.cos(freqs), jnp.sin(freqs))
        q = _rotary(q, cos, sin)
        k = _rotary(k, cos, sin)
        q = jnp.transpose(q, (0, 2, 1, 3)) * HD ** (-0.5)
        k = jnp.repeat(jnp.transpose(k, (0, 2, 1, 3)), NREP, axis=1)
        v = jnp.repeat(jnp.transpose(v, (0, 2, 1, 3)), NREP, axis=1)
        scores = jnp.einsum('bhtd,bhsd->bhts', q, k)
        scores = jnp.nan_to_num(scores)
        mask = jnp.triu(jnp.full((T, T), -jnp.inf, scores.dtype), 1)
        scores = scores + mask
        p = jax.nn.softmax(scores.astype(jnp.float32), axis=-1).astype(scores.dtype)
        lam1 = jnp.exp(jnp.sum(lam_q1 * lam_k1))
        lam2 = jnp.exp(jnp.sum(lam_q2 * lam_k2))
        lam = lam1 - lam2 + LAMBDA_INIT
        p = p.reshape(B, H, 2, T, T)
        diff = p[:, :, 0] - lam * p[:, :, 1]
        attn = jnp.einsum('bhts,bhsd->bhtd', diff, v)
        attn = attn * jax.lax.rsqrt(jnp.mean(attn * attn, axis=-1, keepdims=True) + EPS) * g
        attn = attn * (1.0 - LAMBDA_INIT)
        attn = jnp.transpose(attn, (0, 2, 1, 3)).reshape(B, T, E)
        return attn @ Wo

    def _L0_ffn_ref(hidden_states, router_w, gate_up_proj, down_proj, shared_gate_w, shared_up_w, shared_down_w):
        import jax, jax.numpy as jnp
        import numpy as np
        E, H, I = (8, 256, 512)
        TOP_K = 1
        B, S = (1, 256)
        orig_shape = hidden_states.shape
        x = hidden_states.reshape(-1, H)
        T = x.shape[0]
        logits = x @ router_w.T
        top_vals, top_idx = jax.lax.top_k(logits, TOP_K)
        scores = jnp.full_like(logits, -jnp.inf)
        scores = scores.at[jnp.arange(T)[:, None], top_idx].set(top_vals)
        scores = jax.nn.sigmoid(scores.astype(jnp.float32)).astype(logits.dtype)
        xr = x[None, :, :] * scores.T[:, :, None]
        gate_up = jnp.einsum('eth,ehf->etf', xr, gate_up_proj)
        gate, up = jnp.split(gate_up, 2, axis=-1)
        routed = jnp.einsum('etf,efh->eth', up * jax.nn.silu(gate), down_proj)
        routed_sum = routed.sum(axis=0)
        shared = jax.nn.silu(x @ shared_gate_w) * (x @ shared_up_w) @ shared_down_w
        return (shared + routed_sum).reshape(orig_shape)
    x = L0_attn_x
    x = x + 0.5 * _L0_ffn_ref(_layernorm(x, axis=-1), L0_ffn_router_w, L0_ffn_gate_up_proj, L0_ffn_down_proj, L0_ffn_shared_gate_w, L0_ffn_shared_up_w, L0_ffn_shared_down_w)
    x = x + _L0_attn_ref(_layernorm(x, axis=-1), L0_attn_Wq, L0_attn_Wk, L0_attn_Wv, L0_attn_Wo, L0_attn_lam_q1, L0_attn_lam_k1, L0_attn_lam_q2, L0_attn_lam_k2, L0_attn_g)
    x = x + 0.5 * _L0_ffn_ref(_layernorm(x, axis=-1), L0_ffn_router_w, L0_ffn_gate_up_proj, L0_ffn_down_proj, L0_ffn_shared_gate_w, L0_ffn_shared_up_w, L0_ffn_shared_down_w)
    return x

_drawn_inputs = setup_inputs


def setup_inputs(seed=0):
    import zlib

    import numpy as np

    out = dict(_drawn_inputs(seed))
    spreads = {'L0_attn_g': (1.0, 0.2)}
    factors = {'L0_attn_lam_q1': 8.0,
     'L0_attn_lam_k1': 8.0,
     'L0_attn_lam_q2': 4.783,
     'L0_attn_lam_k2': 4.322,
     'L0_ffn_router_w': 6.94,
     'L0_ffn_gate_up_proj': 6.435,
     'L0_ffn_down_proj': 6.404}
    for name, (base, spread) in spreads.items():
        noise = np.random.default_rng([zlib.crc32(name.encode()), seed]).standard_normal(out[name].shape)
        drawn = base * np.exp(spread * noise) if base else spread * noise
        out[name] = jnp.asarray(drawn.astype(out[name].dtype))
    for name, factor in factors.items():
        out[name] = (out[name] * factor).astype(out[name].dtype)
    return out
```

```python
from contextlib import ExitStack
import math

import concourse.bass as bass
from concourse import mybir

ALU = mybir.AluOpType
ACT = mybir.ActivationFunctionType
AX_X = mybir.AxisListType.X
F32 = mybir.dt.float32
F32R = mybir.dt.float32r
BF16 = mybir.dt.bfloat16
I32 = mybir.dt.int32
U32 = mybir.dt.uint32

P = 128
BATCH, SEQ, DIM = 4, 256, 256
TILES = BATCH * SEQ // P
HALVES = SEQ // P
KC = DIM // P
EXPERTS, INNER = 8, 512
SHARED = EXPERTS
FC = INNER // P
ROUTED_MAX = TILES + EXPERTS - 1
ROUTED_SLOTS = ROUTED_MAX + 1
SLOT_TILES = ROUTED_SLOTS + TILES
HEADS, KV_HEADS = 16, 8
QSUB, KSUB = 2 * HEADS, 2 * KV_HEADS
HD = DIM // HEADS // 2
VD = 2 * HD
SLOT = 32
GROUPS = QSUB // 4
SPAN = 3 * P
LN_EPS, RMS_EPS = 1e-5, 1e-6
LAMBDA_INIT = 0.8 - 0.6 * math.exp(-0.3 * 12)
LAG_B, LAG_PV, LAG_O = 2, 3, 4
SETS = 3
ROWS_A, ROWS_B = 3 * HD, 3 * HD + 2
TURNS = TILES // 2
LESS = (0, 1, TILES, TILES + 1)
N_CONST = 19
N_SMALL = 8 + P // VD
POOL_STEPS = HALVES * 13 + GROUPS + 1
DVE_STEPS = 5
QK_LIMIT = 2.0 ** 60
N_QKV = DIM + 2 * KV_HEADS * VD


def bass_macaron(nc, x_in, wq, wk, wv, wo, lam_q1, lam_k1, lam_q2, lam_k2, g, router_t, gate_up,
                 down, sh_gate, sh_up, sh_down, ident_in, tables_in, rope_in, out):
    x_rows = x_in.rearrange("b (i p) d -> (b i p) d", p=P)
    out_rows = out.rearrange("b (i p) d -> (b i p) d", p=P)
    with ExitStack() as ctx:
        def sb(name, shape, dt=F32):
            return ctx.enter_context(nc.sbuf_tensor(name, shape, dt))

        def sem(name):
            return ctx.enter_context(nc.semaphore(name))

        w_gu = sb("w_gu", [P, EXPERTS + 1, KC, 2 * INNER])
        w_dn = sb("w_dn", [P, EXPERTS + 1, FC, DIM])
        w_qkv = sb("w_qkv", [P, KC, N_QKV])
        w_o = sb("w_o", [P, KC, DIM])
        w_rt = sb("w_rt", [P, KC, EXPERTS])
        ident = sb("ident", [P, P])
        tables = sb("tables", [P, 4, P], BF16)
        ident_b, mask_ts, mask_st, before = (tables[:, n, :] for n in range(4))
        ones_b = sb("ones_b", [P, P], BF16)
        rope = sb("rope", [P, HALVES, 2, HD])
        iota8 = sb("iota8", [P, EXPERTS])
        steps = sb("steps", [P, ROUTED_MAX + 1])
        steps_128 = sb("steps_128", [P, TILES])
        ones8 = sb("ones8", [P, EXPERTS])
        minus_half = sb("minus_half", [P, 2 * HEADS])
        lam_in = sb("lam_in", [P, 4, HD])
        lam_pr = sb("lam_pr", [P, 2, HD])
        lam_s = sb("lam_s", [P, 2])
        lam_e = sb("lam_e", [P, 2])
        neg_lam = sb("neg_lam", [P, 1])
        g_col = sb("g_col", [P, 1])
        x_res = sb("x_res", [P, TILES, DIM])
        xn = sb("xn", [P, TILES, DIM])
        moved = sb("moved", [P, TILES, DIM])
        stats = sb("stats", [P, TILES, 6])
        mean_var = sb("mean_var", [P, TILES, 2])
        var_eps = sb("var_eps", [P, TILES])
        rstd = sb("rstd", [P, TILES])
        xn_t = sb("xn_t", [P, TILES, KC, P])
        top = sb("top", [P, TILES])
        score = sb("score", [P, TILES])
        is_top = sb("is_top", [P, TILES, EXPERTS])
        key = sb("key", [P, TILES, EXPERTS])
        pick = sb("pick", [P, TILES])
        onehot = sb("onehot", [P, TILES, EXPERTS])
        onehot_b = sb("onehot_b", [P, TILES, EXPERTS], BF16)
        count = sb("count", [P, EXPERTS])
        over = sb("over", [P, EXPERTS, TILES])
        e_tiles = sb("e_tiles", [P, EXPERTS])
        e_end = sb("e_end", [P, EXPERTS])
        e_start = sb("e_start", [P, EXPERTS])
        pos = sb("pos", [P, TILES])
        pos_u = sb("pos_u", [P, TILES], U32)
        t_exp = sb("t_exp", [P, ROUTED_MAX + 1])
        tile_expert = sb("tile_expert", [P, TILES + ROUTED_SLOTS], I32)
        n_base = sb("n_base", [P, len(LESS)])
        n_tiles = sb("n_tiles", [P, len(LESS)], I32)
        x_tile = sb("x_tile", [P, DIM])
        x_t = sb("x_t", [P, KC, P])
        work = sb("work", [P, 4, INNER])
        act_g, hid = work[:, 0, :], work[:, 1, :]
        hid_t = work[:, 2, :].rearrange("p (c t) -> p c t", t=P)
        y_tile = sb("y_tile", [P, DIM])
        past = work[:, 3, 0:P].rearrange("p (t e) -> p t e", e=EXPERTS)
        place = work[:, 3, P:P + TILES * EXPERTS].rearrange("p (t e) -> p t e", e=EXPERTS)
        place2 = work[:, 3, 2 * P:2 * P + TILES * EXPERTS].rearrange("p (t e) -> p t e", e=EXPERTS)
        zero_row = y_tile
        q_all = xn[:].rearrange("p t (n d) -> p t n d", d=HD)
        kv_all = xn_t[:].rearrange("p t c m -> p t (c m)")
        v_now = sb("v_now", [P, HALVES, KV_HEADS, SLOT])
        rot_a = work[:, 2, 0:(QSUB + KSUB) * HD].rearrange("p (n d) -> p n d", d=HD)
        rot_b = work[:, 3, 0:(QSUB + KSUB) * HD].rearrange("p (n d) -> p n d", d=HD)
        q_pad = sb("q_pad", [P, HALVES, QSUB, SLOT])
        k_pad = sb("k_pad", [P, HALVES, KSUB, 2, SLOT])
        qk_t = sb("qk_t", [P, 4, 2, SEQ], F32R)
        qm_t = sb("qm_t", [P, 2, SEQ], F32R)
        blk_max = sb("blk_max", [P, QSUB, 4])
        probs = sb("probs", [P, 4, 2, SPAN])
        o_t = x_t[:].rearrange("p c t -> p (c t)")
        o_tok = sb("o_tok", [P, HALVES, QSUB, VD + 1])
        neg_max = sb("neg_max", [P, HALVES, QSUB])
        o_inv = sb("o_inv", [P, HALVES * QSUB])
        o_dif = work[:, 0, :].rearrange("p (n d) -> p n d", d=VD)
        o_sq = work[:, 1, :].rearrange("p (n d) -> p n d", d=VD)
        o_ms = sb("o_ms", [P, HALVES * HEADS])
        o_me = sb("o_me", [P, HALVES * HEADS])
        o_rs = sb("o_rs", [P, HALVES * HEADS])
        attn = moved

        ps = ctx.enter_context(nc.psum_tensor("ps", [P, 8, 512], F32))
        B_GATE, B_UP, B_HT, B_XT, B_Y, B_LOGIT, B_RANK, B_COUNT = range(8)
        B_TURN = (B_HT, B_XT)
        B_MISC, B_O = 6, 7

        slots_x = nc.dram_tensor("slots_x", (SLOT_TILES * P, DIM), F32).ap()
        slots_y = nc.dram_tensor("slots_y", (ROUTED_SLOTS * P, DIM), F32).ap()
        routed_x, shared_x = slots_x[0:ROUTED_SLOTS * P, :], slots_x[ROUTED_SLOTS * P:, :]

        order = []
        for u in range(GROUPS + LAG_O):
            if u < GROUPS:
                order += [("A", u, 0), ("A", u, 1)]
            if 0 <= u - LAG_B < GROUPS:
                order += [("B", u - LAG_B, 0), ("B", u - LAG_B, 1)]
        score_set = {unit: n % SETS for n, unit in enumerate(order)}
        set_before = {unit: order[n - SETS] if n >= SETS else None for n, unit in enumerate(order)}
        misc_order = [("QK", 0)]
        for u in range(GROUPS + LAG_O):
            misc_order += [(kind, g) for kind, g in (("QK", u + 1), ("QM", u - LAG_B), ("O", u - LAG_O))
                           if 0 <= g < GROUPS]
        UNITS = 2 * GROUPS

        s_x = sem("x_loaded")
        s_small = sem("small_loaded")
        s_wsh = sem("shared_weights_loaded")
        s_wex = sem("expert_weights_loaded")
        s_watt = sem("attention_weights_loaded")
        s_tables = sem("tables_ready")
        s_const = sem("pool_constants")
        s_zero = sem("slots_zeroed")
        s_lam = sem("lambda_steps")
        s_lame = sem("lambda_exps")
        s_dve = sem("dve_chain")
        s_pool = sem("pool_chain")
        s_stat = sem("ln_stats")
        s_mv = sem("ln_mean_var")
        s_rstd = sem("ln_rstd")
        s_xn = sem("xn_ready")
        s_turn = sem("tiles_turned")
        s_turned = sem("turned_tiles_copied")
        s_res = sem("residual_updated")
        s_out = sem("out_stored")

        s_qkv = sem("qkv_done")
        s_qkvc = sem("qkv_copied")
        s_pad = sem("qk_split")
        s_vnow = sem("v_ready")
        s_fill = sem("qk_turned")
        s_filc = sem("qk_turned_copied")
        s_ascore = sem("row_scores_done")
        s_max = sem("row_max_done")
        s_row = sem("neg_row_max_ready")
        s_neg = sem("neg_max_ready")
        s_qm = sem("q_max_turned")
        s_qmc = sem("q_max_copied")
        s_bscore = sem("column_scores_done")
        s_exp = sem("exp_done")
        s_pv = sem("pv_done")
        s_oc = sem("o_copied")
        s_ot = sem("o_turned")
        s_otc = sem("o_tokens_copied")
        s_ms = sem("o_square_sums")
        s_rs = sem("o_rstd")
        s_attn = sem("attn_ready")
        s_passed = sem("pool_waits_passed")
        s_pin = sem("pool_loop_chain")
        s_din = sem("dve_loop_chain")
        s_wo = sem("wo_scaled")
        s_proj = sem("projected")

        block = ctx.enter_context(nc.Block())
        names = ("xn_stored", "logits_done", "top_ready", "score_ready", "onehot_ready", "ranks_done",
                 "scaled_ready", "pos_ready", "plan_ready", "scattered", "tile_loaded", "tile_turned",
                 "tile_t_ready", "gate_up_done", "silu_done", "hidden_ready", "hidden_turned",
                 "hidden_t_ready", "y_done", "y_ready", "y_stored", "gathered")
        ffn = [{n: sem(f"{n}_{k}") for n in names} for k in range(2)]

        class Chain:

            def __init__(self, eng, s, base=0, passed=None):
                self.eng, self.s, self.base, self.passed, self.n = eng, s, base, passed, 0

            def step(self, ins):
                self.n += 1
                ins.then_inc(self.s, 1)
                self.eng.wait_ge(self.s, self.base + self.n)
                if self.passed is not None:
                    self.eng.sem_inc(self.passed, 1)

        def one(t, j):
            return t[:, bass.ds(j, 1), :].rearrange("p a d -> p (a d)")

        def tile_count(eng, less=0):
            at = LESS.index(less)
            return eng.value_load(n_tiles[0:1, at:at + 1], min_val=2 * TILES - less,
                                  max_val=TILES + ROUTED_MAX - less)

        @block.sync
        def _(sp):
            for j in range(TILES):
                sp.dma_start(x_res[:, j, :], x_rows[j * P:(j + 1) * P, :]).then_inc(s_x, 16)
            sp.dma_start(ident[:], ident_in).then_inc(s_small, 16)
            sp.dma_start(work[:, 0, :], tables_in.rearrange("p n m -> p (n m)")).then_inc(s_small, 16)
            sp.dma_start(w_rt[:], router_t.rearrange("(c p) e -> p c e", p=P)).then_inc(s_small, 16)
            sp.dma_start(rope[:], rope_in.rearrange("(i p) a d -> p i a d", p=P)).then_inc(s_small, 16)
            for n, v in enumerate((lam_q1, lam_k1, lam_q2, lam_k2)):
                sp.dma_start(lam_in[:, n, :], v.rearrange("(a d) -> a d", a=1).to_broadcast([P, HD]))\
                    .then_inc(s_small, 16)
            for h in range(P // VD):
                sp.dma_start(g_col[h * VD:(h + 1) * VD, :], g.rearrange("(d a) -> d a", a=1))\
                    .then_inc(s_small, 16)
            sp.wait_ge(s_const, 1)
            for slots in (routed_x, slots_y):
                sp.dma_start(slots.rearrange("(i p) d -> p i d", p=P),
                             zero_row[:].unsqueeze(1).to_broadcast([P, ROUTED_SLOTS, DIM]))\
                    .then_inc(s_zero, 16)
            for k in range(2):
                s = ffn[k]
                with sp.Fori(0, TILES) as j:
                    sp.wait_ge(s_xn, 2 * k * TILES + j + 1)
                    sp.dma_start(shared_x[bass.ds(j * P, P), :], one(xn, j))\
                        .then_inc(s["xn_stored"], 16)
                sp.wait_ge(s["xn_stored"], 16 * TILES)
                sp.dma_start(x_tile[:], shared_x[0:P, :]).then_inc(s["tile_loaded"], 16)
                sp.wait_ge(s["tile_turned"], 1)
                sp.dma_start(x_tile[:], shared_x[P:2 * P, :]).then_inc(s["tile_loaded"], 16)
                with sp.Fori(1, TILES - 1) as i:
                    sp.wait_ge(s["tile_turned"], i + 1)
                    sp.dma_start(x_tile[:], shared_x[bass.ds((i + 1) * P, P), :])\
                        .then_inc(s["tile_loaded"], 16)
                sp.wait_ge(s["scattered"], 16 * TILES)
                sp.wait_ge(s["plan_ready"], 2)
                routed, last = tile_count(sp, TILES), tile_count(sp, TILES + 1)
                for r in range(2):
                    sp.wait_ge(s["tile_turned"], TILES + r)
                    sp.dma_start(x_tile[:], routed_x[r * P:(r + 1) * P, :]).then_inc(s["tile_loaded"], 16)
                with sp.Fori(1, routed) as r:
                    sp.wait_ge(s["tile_turned"], r + (TILES + 1))
                    sp.dma_start(x_tile[:], routed_x[bass.ds((r + 1) * P, P), :])\
                        .then_inc(s["tile_loaded"], 16)
                    sp.wait_ge(s["y_ready"], r + TILES)
                    sp.dma_start(slots_y[bass.ds((r - 1) * P, P), :], y_tile[:])\
                        .then_inc(s["y_stored"], 16)
                sp.wait_ge(s["y_ready"], routed + TILES)
                sp.dma_start(slots_y[bass.ds(last * P, P), :], y_tile[:])\
                    .then_inc(s["y_stored"], 16)
            with sp.Fori(0, TILES) as j:
                sp.wait_ge(s_res, 2 * TILES + j + 1)
                sp.dma_start(out_rows[bass.ds(j * P, P), :], one(x_res, j)).then_inc(s_out, 16)
            sp.wait_ge(s_out, 16 * TILES)

        @block.gpsimd
        def _(pool):
            chain = Chain(pool, s_pool)
            pool.memset(zero_row[:], 0.0).then_inc(s_const, 1)
            pool.memset(ones_b[:], 1.0).then_inc(s_const, 1)
            pool.memset(ones8[:], 1.0).then_inc(s_const, 1)
            pool.memset(minus_half[:], -0.5).then_inc(s_const, 1)
            pool.iota(iota8[:], [[1, EXPERTS]], base=-EXPERTS, channel_multiplier=0,
                      allow_small_or_imprecise_dtypes=True).then_inc(s_const, 1)
            pool.iota(steps[:], [[1, ROUTED_MAX + 1]], base=0, channel_multiplier=0,
                      allow_small_or_imprecise_dtypes=True).then_inc(s_const, 1)
            pool.iota(steps_128[:], [[P, TILES]], base=0, channel_multiplier=0,
                      allow_small_or_imprecise_dtypes=True).then_inc(s_const, 1)
            pool.memset(blk_max[:, :, 0:1], 3e38).then_inc(s_const, 1)
            for at, less in enumerate(LESS):
                pool.memset(n_base[:, at:at + 1], float(TILES - less)).then_inc(s_const, 1)
            pool.memset(q_pad[:], 0.0).then_inc(s_const, 1)
            pool.memset(k_pad[:], 0.0).then_inc(s_const, 1)
            pool.memset(v_now[:], 0.0).then_inc(s_const, 1)
            pool.wait_ge(s_const, 15)
            for i in range(HALVES):
                pool.memset(k_pad[:, i].rearrange("p k u s -> p (k u) s")[:, :, ROWS_A:ROWS_B], 1.0)\
                    .then_inc(s_const, 1)
                pool.memset(v_now[:, i, :, VD:VD + 1], 1.0).then_inc(s_const, 1)
            pool.wait_ge(s_const, N_CONST)

            def loop_wait(s, value):
                pool.wait_ge(s, value)
                pool.sem_inc(s_passed, 1)

            def rstds(n):
                pool.wait_ge(s_mv, TILES * (n + 1))
                chain.step(pool.tensor_scalar(var_eps[:], mean_var[:, :, 1], LN_EPS, None, ALU.add))
                pool.tensor_tensor(rstd[:], var_eps[:], minus_half[:, 0:TILES], ALU.pow)\
                    .then_inc(s_rstd, 1)

            def route(k):
                s = ffn[k]
                pool.wait_ge(s["pos_ready"], 1)
                pool.wait_ge(s["scaled_ready"], TILES)
                if k == 0:
                    pool.wait_ge(s_zero, 16 * 2)
                for j in range(TILES):
                    pool.indirect_dma_start(
                        out=slots_x, out_offset=bass.IndirectOffsetOnAxis(ap=pos_u[:, j:j + 1], axis=0),
                        in_=moved[:, j, :], in_offset=None).then_inc(s["scattered"], 16)
                pool.wait_ge(s["plan_ready"], 2)
                routed = tile_count(pool, TILES)
                pool.wait_ge(s["scattered"], 16 * TILES)
                loop_wait(s["y_stored"], routed * 16)
                for j in range(TILES):
                    pool.indirect_dma_start(
                        out=moved[:, j, :], out_offset=None, in_=slots_y,
                        in_offset=bass.IndirectOffsetOnAxis(ap=pos_u[:, j:j + 1], axis=0))\
                        .then_inc(s["gathered"], 16)

            def attention(b):
                own = Chain(pool, s_pin, b * POOL_STEPS, s_passed)
                for i in range(HALVES):
                    q_in = one(xn, b * HALVES + i).rearrange("p (n d) -> p n d", d=HD)
                    k_in = one(kv_all, b * HALVES + i)[:, 0:KSUB * HD].rearrange("p (n d) -> p n d", d=HD)
                    cos, sin = rope[:, i, 0:1, :], rope[:, i, 1:2, :]
                    low, high = slice(0, HD // 2), slice(HD // 2, HD)
                    for t, at, n in ((q_in, 0, QSUB), (k_in, QSUB, KSUB)):
                        r = slice(at, at + n)
                        pool.tensor_tensor(rot_a[:, r, :], t, cos.to_broadcast([P, n, HD]), ALU.mult)\
                            .then_inc(s_pin, 1)
                        pool.tensor_tensor(rot_b[:, r, low], t[:, :, high],
                                           sin[:, :, low].to_broadcast([P, n, HD // 2]), ALU.mult)\
                            .then_inc(s_pin, 1)
                        own.n += 2
                        own.step(pool.tensor_tensor(rot_b[:, r, high], t[:, :, low],
                                                    sin[:, :, high].to_broadcast([P, n, HD // 2]),
                                                    ALU.mult))
                    own.step(pool.tensor_tensor(rot_a, rot_a, rot_b, ALU.add))
                    q, k = rot_a[:, 0:QSUB, :], rot_a[:, QSUB:QSUB + KSUB, :]
                    pool.tensor_copy(q_pad[:, i, :, 0:HD].bitcast(F32R), q).then_inc(s_pin, 1)
                    pool.tensor_copy(q_pad[:, i, :, 2 * HD:3 * HD].bitcast(F32R), q).then_inc(s_pin, 1)
                    own.n += 2
                    for u in range(2):
                        for h in range(2):
                            ins = pool.tensor_copy(
                                k_pad[:, i, :, u, h * HD:(h + 1) * HD].bitcast(F32R), k)
                            if (u, h) != (1, 1):
                                ins.then_inc(s_pin, 1)
                                own.n += 1
                    own.step(ins)
                    for u in range(2):
                        pool.tensor_tensor(k_pad[:, i, :, u, 2 * HD:3 * HD], k,
                                           k_pad[:, i, :, u, 0:HD], ALU.subtract).then_inc(s_pad, 1)
                    pool.tensor_tensor(q_pad[:, i, :, HD:2 * HD], q, q_pad[:, i, :, 0:HD],
                                       ALU.subtract).then_inc(s_pad, 1)
                    loop_wait(s_pad, (b * HALVES + i + 1) * 3)
                for i in range(HALVES):
                    pool.tensor_copy(v_now[:, i, :, 0:VD],
                                     one(kv_all, b * HALVES + i)[:, KSUB * HD:]
                                     .rearrange("p (n d) -> p n d", d=VD)).then_inc(s_vnow, 1)
                for g in range(GROUPS):
                    r = slice(4 * g, 4 * g + 4)
                    loop_wait(s_row, b * GROUPS + g + 1)
                    own.step(pool.tensor_copy(q_pad[:, :, r, ROWS_A].bitcast(F32R), neg_max[:, :, r]))
                    pool.tensor_tensor(q_pad[:, :, r, ROWS_A + 1], neg_max[:, :, r],
                                       q_pad[:, :, r, ROWS_A], ALU.subtract).then_inc(s_neg, 1)
                loop_wait(s_ms, b + 1)
                own.step(pool.tensor_scalar(o_me[:], o_ms[:], 1.0 / VD, RMS_EPS, ALU.mult, ALU.add))
                pool.tensor_tensor(o_rs[:], o_me[:], minus_half[:], ALU.pow).then_inc(s_rs, 1)
                assert own.n == POOL_STEPS, own.n

            rstds(0)
            route(0)
            rstds(1)
            pool.wait_ge(s_small, 16 * N_SMALL)
            pool.wait_ge(s_qkvc, 3 * TILES)
            with pool.Fori(0, BATCH) as b:
                attention(b)
            rstds(2)
            route(1)

        @block.vector
        def _(dve):
            chain = Chain(dve, s_dve)

            def layernorm(n):
                if n == 0:
                    dve.wait_ge(s_x, 16 * TILES)
                else:
                    dve.wait_ge(s_res, n * TILES)
                with dve.Fori(0, TILES) as j:
                    dve.bn_stats(one(stats, j), one(x_res, j)).then_inc(s_stat, 1)
                dve.wait_ge(s_stat, (n + 1) * TILES)
                for j in range(TILES):
                    dve.bn_aggr(mean_var[:, j, :], stats[:, j, :]).then_inc(s_mv, 1)
                dve.wait_ge(s_rstd, n + 1)
                dve.wait_ge(s_mv, (n + 1) * TILES)
                for j in range(TILES):
                    dve.tensor_scalar(xn[:, j, :], x_res[:, j, :], mean_var[:, j, 0:1],
                                      rstd[:, j:j + 1], ALU.subtract, ALU.mult).then_inc(s_xn, 1)

            def plan(k):
                s = ffn[k]
                full = [P, TILES, EXPERTS]
                logits = ps[:, B_LOGIT, 0:TILES * EXPERTS].rearrange("p (t e) -> p t e", e=EXPERTS)
                rank = ps[:, B_RANK, 0:TILES * EXPERTS].rearrange("p (t e) -> p t e", e=EXPERTS)
                dve.wait_ge(s["logits_done"], 1)
                dve.tensor_reduce(top[:], logits, AX_X, ALU.max).then_inc(s["top_ready"], 1)
                dve.wait_ge(s["top_ready"], 1)
                chain.step(dve.tensor_tensor(is_top[:], logits, top[:].unsqueeze(2).to_broadcast(full),
                                             ALU.is_equal))
                chain.step(dve.scalar_tensor_tensor(key[:], is_top[:], -float(EXPERTS),
                                                    iota8[:].unsqueeze(1).to_broadcast(full),
                                                    ALU.mult, ALU.add))
                chain.step(dve.tensor_reduce(pick[:], key[:], AX_X, ALU.min))
                dve.tensor_tensor(onehot_b[:], key[:], pick[:].unsqueeze(2).to_broadcast(full),
                                  ALU.is_equal).then_inc(s["onehot_ready"], 1)
                dve.wait_ge(s["score_ready"], 1)
                for j in range(TILES):
                    dve.tensor_scalar(moved[:, j, :], xn[:, j, :], score[:, j:j + 1], None, ALU.mult)\
                        .then_inc(s["scaled_ready"], 1)
                dve.wait_ge(s["ranks_done"], 1)
                chain.step(dve.tensor_copy(count[:], ps[:, B_COUNT, 0:EXPERTS]))
                chain.step(dve.tensor_tensor(over[:], count[:].unsqueeze(2).to_broadcast([P, EXPERTS, TILES]),
                                             steps_128[:].unsqueeze(1).to_broadcast([P, EXPERTS, TILES]),
                                             ALU.is_gt))
                chain.step(dve.tensor_reduce(e_tiles[:], over[:], AX_X, ALU.add))
                chain.step(dve.tensor_tensor_scan(e_end[:], ones8[:], e_tiles[:], 0.0, ALU.mult, ALU.add))
                chain.step(dve.tensor_tensor(e_start[:], e_end[:], e_tiles[:], ALU.subtract))
                chain.step(dve.scalar_tensor_tensor(place, e_start[:].unsqueeze(1).to_broadcast(full),
                                                    float(P), rank, ALU.mult, ALU.add))
                chain.step(dve.tensor_tensor(place2, place, onehot_b[:], ALU.mult))
                chain.step(dve.tensor_reduce(pos[:], place2, AX_X, ALU.add))
                dve.tensor_copy(pos_u[:], pos[:]).then_inc(s["pos_ready"], 1)
                wide = [P, ROUTED_MAX + 1, EXPERTS]
                chain.step(dve.tensor_tensor(past, e_end[:].unsqueeze(1).to_broadcast(wide),
                                             steps[:].unsqueeze(2).to_broadcast(wide), ALU.is_le))
                chain.step(dve.tensor_reduce(t_exp[:], past, AX_X, ALU.add))
                dve.tensor_scalar(tile_expert[:, TILES:], t_exp[:], float(EXPERTS - 1), None,
                                  ALU.min).then_inc(s["plan_ready"], 1)
                dve.tensor_scalar(n_tiles[:], n_base[:], e_end[:, EXPERTS - 1:EXPERTS], None,
                                  ALU.add).then_inc(s["plan_ready"], 1)

            def experts(k):
                s = ffn[k]

                def turned(i):
                    dve.wait_ge(s["tile_turned"], i + 1)
                    dve.wait_ge(s["gate_up_done"], i)
                    dve.tensor_copy(x_t[:], ps[:, B_XT, 0:DIM].rearrange("p (c t) -> p c t", t=P))\
                        .then_inc(s["tile_t_ready"], 1)

                def hidden(i):
                    dve.wait_ge(s["silu_done"], i + 1)
                    dve.wait_ge(s["hidden_turned"], i)
                    dve.tensor_tensor(hid, act_g, ps[:, B_UP, :], ALU.mult)\
                        .then_inc(s["hidden_ready"], 1)

                def add_shared(i, x):
                    dve.wait_ge(s["y_done"], i + 1)
                    dve.scalar_tensor_tensor(x, ps[:, B_Y, 0:DIM], 0.5, x, ALU.mult, ALU.add)\
                        .then_inc(s["y_ready"], 1)

                def copy_routed(i):
                    dve.wait_ge(s["y_done"], i + 1)
                    dve.tensor_copy(y_tile[:], ps[:, B_Y, 0:DIM]).then_inc(s["y_ready"], 1)

                turned(0)
                turned(1)
                hidden(0)
                with dve.Fori(1, TILES) as i:
                    turned(i + 1)
                    hidden(i)
                    add_shared(i - 1, one(x_res, i - 1))
                turned(TILES + 1)
                hidden(TILES)
                add_shared(TILES - 1, x_res[:, TILES - 1, :])
                n = tile_count(dve)
                turned(TILES + 2)
                hidden(TILES + 1)
                copy_routed(TILES)
                with dve.Fori(TILES + 2, n) as i:
                    turned(i + 1)
                    hidden(i)
                    dve.wait_ge(s["y_stored"], (i - (TILES + 1)) * 16)
                    copy_routed(i - 1)
                dve.wait_ge(s["y_stored"], tile_count(dve, TILES + 1) * 16)
                dve.wait_ge(s["y_done"], n)
                dve.tensor_copy(y_tile[:], ps[:, B_Y, 0:DIM]).then_inc(s["y_ready"], 1)
                dve.wait_ge(s["gathered"], 16 * TILES)
                for j in range(TILES):
                    dve.scalar_tensor_tensor(x_res[:, j, :], moved[:, j, :], 0.5, x_res[:, j, :],
                                             ALU.mult, ALU.add).then_inc(s_res, 1)

            def qkv():
                for j in range(TILES):
                    bank = ps[:, j % 2, :]
                    dve.wait_ge(s_qkv, j + 1)
                    dve.tensor_scalar(xn[:, j, :], bank[:, 0:DIM], QK_LIMIT, -QK_LIMIT, ALU.min, ALU.max)\
                        .then_inc(s_qkvc, 1)
                    dve.tensor_scalar(kv_all[:, j, 0:KSUB * HD], bank[:, DIM:DIM + KSUB * HD],
                                      QK_LIMIT, -QK_LIMIT, ALU.min, ALU.max).then_inc(s_qkvc, 1)
                    dve.tensor_copy(kv_all[:, j, KSUB * HD:], bank[:, DIM + KSUB * HD:N_QKV])\
                        .then_inc(s_qkvc, 1)

            def row_max(b, g):
                for h in range(2):
                    st = score_set["A", g, h]
                    dve.wait_ge(s_ascore, b * UNITS + 2 * g + h + 1)
                    dve.tensor_reduce(blk_max[:, 4 * g + 2 * h:4 * g + 2 * h + 2, 1:4],
                                      ps[:, 2 * st:2 * st + 2, 0:SPAN].rearrange("p a (c k) -> p a c k", k=P),
                                      AX_X, ALU.max, negate=True).then_inc(s_max, 1)
                r = slice(4 * g, 4 * g + 4)
                dve.wait_ge(s_max, b * UNITS + 2 * g + 2)
                dve.tensor_reduce(neg_max[:, :, r].rearrange("p i r -> p r i"),
                                  blk_max[:, r, :].rearrange("p r (i two) -> p r i two", two=2),
                                  AX_X, ALU.min).then_inc(s_row, 1)

            def o_tokens(b, g):
                dve.wait_ge(s_ot, b * GROUPS + g + 1)
                dve.tensor_copy(o_tok[:, :, 4 * g:4 * g + 4, :],
                                ps[:, B_MISC, 0:SEQ].rearrange("p (i r d) -> p i r d", i=HALVES, d=SLOT)
                                [:, :, :, 0:VD + 1]).then_inc(s_otc, 1)

            def attention(b):
                own = Chain(dve, s_din, b * DVE_STEPS)
                for u in range(GROUPS + LAG_O):
                    if u < GROUPS:
                        row_max(b, u)
                    if u >= LAG_O:
                        o_tokens(b, u - LAG_O)
                dve.wait_ge(s_otc, (b + 1) * GROUPS)
                o = o_tok[:].rearrange("p i n d -> p (i n) d")
                both = [P, HALVES * QSUB, VD]
                half = [P, HALVES * HEADS, VD]
                own.step(dve.reciprocal(o_inv[:], o[:, :, VD]))
                odd = o_inv[:].rearrange("p (n two) -> p n two", two=2)[:, :, 1]
                own.step(dve.tensor_scalar(odd, odd, neg_lam[:], None, ALU.mult))
                own.step(dve.tensor_tensor(o[:, :, 0:VD], o[:, :, 0:VD],
                                           o_inv[:].unsqueeze(2).to_broadcast(both), ALU.mult))
                pair = o.rearrange("p (n two) d -> p n two d", two=2)[:, :, :, 0:VD]
                own.step(dve.tensor_tensor(o_dif, pair[:, :, 0, :], pair[:, :, 1, :], ALU.add))
                own.step(dve.tensor_tensor(o_sq, o_dif, o_dif, ALU.mult))
                dve.tensor_reduce(o_ms[:], o_sq, AX_X, ALU.add).then_inc(s_ms, 1)
                dve.wait_ge(s_rs, b + 1)
                dve.tensor_tensor(attn[:, bass.ds(b * HALVES, HALVES), :]
                                  .rearrange("p i (n d) -> p (i n) d", d=VD),
                                  o_dif, o_rs[:].unsqueeze(2).to_broadcast(half), ALU.mult)\
                    .then_inc(s_attn, 1)
                assert own.n == DVE_STEPS, own.n

            def project():
                for j in range(TILES):
                    dve.wait_ge(s_proj, j + 1)
                    dve.tensor_tensor(x_res[:, j, :], x_res[:, j, :], ps[:, j % 2, 0:DIM], ALU.add)\
                        .then_inc(s_res, 1)

            dve.memset(tile_expert[:, 0:TILES], SHARED).then_inc(s_dve, 1)
            chain.n += 1
            dve.wait_ge(s_const, N_CONST)
            dve.wait_ge(s_small, 16 * N_SMALL)
            dve.tensor_copy(tables[:].rearrange("p n m -> p (n m)"), work[:, 0, :]).then_inc(s_tables, 1)
            layernorm(0)
            plan(0)
            experts(0)
            dve.wait_ge(s_small, 16 * N_SMALL)
            pairs = lam_in[:].rearrange("p (n two) d -> p n two d", two=2)
            chain.step(dve.tensor_tensor(lam_pr[:], pairs[:, :, 0, :], pairs[:, :, 1, :], ALU.mult))
            dve.tensor_reduce(lam_s[:], lam_pr[:], AX_X, ALU.add).then_inc(s_lam, 1)
            dve.wait_ge(s_watt, 16 * 4)
            dve.tensor_scalar(w_o[:], w_o[:], g_col[:], 1.0 - LAMBDA_INIT, ALU.mult, ALU.mult)\
                .then_inc(s_wo, 1)
            dve.wait_ge(s_lame, 1)
            chain.step(dve.scalar_tensor_tensor(neg_lam[:], lam_e[:, 1:2], -LAMBDA_INIT, lam_e[:, 0:1],
                                                ALU.add, ALU.subtract))
            layernorm(1)
            qkv()
            with dve.Fori(0, BATCH) as b:
                attention(b)
            project()
            layernorm(2)
            plan(1)
            experts(1)

        @block.scalar
        def _(act):
            halves = ((sh_gate, 0), (sh_up, INNER))
            for w, at in halves:
                act.dma_start(w_gu[:, SHARED, :, at:at + INNER], w.rearrange("(c p) f -> p c f", p=P))\
                    .then_inc(s_wsh, 16)
            act.dma_start(w_dn[:, SHARED], sh_down.rearrange("(c p) d -> p c d", p=P)).then_inc(s_wsh, 16)
            for e in range(EXPERTS):
                act.dma_start(w_gu[:, e], gate_up[e].rearrange("(c p) f -> p c f", p=P))\
                    .then_inc(s_wex, 16)
                act.dma_start(w_dn[:, e], down[e].rearrange("(c p) d -> p c d", p=P))\
                    .then_inc(s_wex, 16)
            for w, at in ((wq, 0), (wk, DIM), (wv, DIM + KV_HEADS * VD)):
                act.dma_start(w_qkv[:, :, at:at + w.shape[1]], w.rearrange("(c p) n -> p c n", p=P))\
                    .then_inc(s_watt, 16)
            act.dma_start(w_o[:], wo.rearrange("(c p) n -> p c n", p=P)).then_inc(s_watt, 16)

            def turned(n):
                for f in range(TURNS):
                    act.wait_ge(s_turn, n * TURNS + f + 1)
                    act.activation(xn_t[:, 2 * f:2 * f + 2].rearrange("p a c t -> p (a c t)"),
                                   ps[:, B_TURN[f % 2], :], ACT.Copy).then_inc(s_turned, 1)

            def experts(k):
                s = ffn[k]

                def tile(i):
                    act.wait_ge(s["gate_up_done"], i + 1)
                    act.wait_ge(s["hidden_ready"], i)
                    act.activation(act_g, ps[:, B_GATE, :], ACT.Silu).then_inc(s["silu_done"], 1)
                    act.wait_ge(s["hidden_turned"], i + 1)
                    act.wait_ge(s["y_done"], i)
                    act.activation(hid_t.rearrange("p c t -> p (c t)"), ps[:, B_HT, :], ACT.Copy)\
                        .then_inc(s["hidden_t_ready"], 1)

                act.wait_ge(s["top_ready"], 1)
                act.activation(score[:], top[:], ACT.Sigmoid).then_inc(s["score_ready"], 1)
                tile(0)
                with act.Fori(1, TILES) as i:
                    tile(i)
                act.wait_ge(s["plan_ready"], 2)
                n = tile_count(act)
                with act.Fori(TILES, n) as i:
                    tile(i)

            def attention(b):
                def copy_qk(g):
                    act.wait_ge(s_fill, b * GROUPS + g + 1)
                    act.activation(qk_t[:, g % 4].rearrange("p a t -> p (a t)"), ps[:, B_MISC, :], ACT.Copy)\
                        .then_inc(s_filc, 1)

                copy_qk(0)
                for u in range(GROUPS + LAG_O):
                    if u + 1 < GROUPS:
                        copy_qk(u + 1)
                    g = u - LAG_B
                    if 0 <= g < GROUPS:
                        act.wait_ge(s_qm, b * GROUPS + g + 1)
                        if g >= 2:
                            act.wait_ge(s_bscore, b * UNITS + 2 * (g - 1))
                        act.activation(qm_t[:, g % 2, :], ps[:, B_MISC, 0:SEQ], ACT.Copy)\
                            .then_inc(s_qmc, 1)
                        for h in range(2):
                            st = score_set["B", g, h]
                            act.wait_ge(s_bscore, b * UNITS + 2 * g + h + 1)
                            if g >= 2:
                                act.wait_ge(s_pv, b * GROUPS + g - 1)
                            act.activation(probs[:, (2 * g + h) % 4], ps[:, 2 * st:2 * st + 2, 0:SPAN],
                                           ACT.Exp, scale=HD ** -0.5).then_inc(s_exp, 1)
                    g = u - LAG_PV
                    if 0 <= g < GROUPS:
                        act.wait_ge(s_pv, b * GROUPS + g + 1)
                        if g >= 1:
                            act.wait_ge(s_ot, b * GROUPS + g)
                        act.activation(o_t, ps[:, B_O, 0:SEQ], ACT.Copy).then_inc(s_oc, 1)

            turned(0)
            experts(0)
            act.wait_ge(s_lam, 1)
            act.activation(lam_e[:], lam_s[:], ACT.Exp).then_inc(s_lame, 1)
            turned(1)
            with act.Fori(0, BATCH) as b:
                attention(b)
            turned(2)
            turned(3)
            experts(1)

        @block.tensor
        def _(pe):
            def turn(n, src, ready):
                for f in range(TURNS):
                    ready(f)
                    if n * TURNS + f >= 2:
                        pe.wait_ge(s_turned, n * TURNS + f - 1)
                    for m in range(2 * KC):
                        j, c = 2 * f + m // KC, m % KC
                        ins = pe.transpose(ps[:, B_TURN[f % 2], m * P:(m + 1) * P],
                                           src[:, j, c * P:(c + 1) * P], ident[:])
                    ins.then_inc(s_turn, 1)

            def ln_ready(n):
                return lambda f: pe.wait_ge(s_xn, n * TILES + 2 * f + 2)

            def route(k):
                s = ffn[k]
                n = (0, 3)[k]
                pe.wait_ge(s_turned, (n + 1) * TURNS)
                for j in range(TILES):
                    for c in range(KC):
                        ins = pe.matmul(ps[:, B_LOGIT, j * EXPERTS:(j + 1) * EXPERTS], xn_t[:, j, c, :],
                                        w_rt[:, c, :], start=(c == 0), stop=(c == KC - 1))
                ins.then_inc(s["logits_done"], 1)
                pe.wait_ge(s["onehot_ready"], 1)
                for d in range(TILES):
                    pe.matmul(ps[:, B_RANK, d * EXPERTS:TILES * EXPERTS], before if d == 0 else ones_b[:],
                              onehot_b[:, 0:TILES - d].rearrange("p t e -> p (t e)"),
                              start=(d == 0), stop=(d == TILES - 1), skip_group_check=True)
                for j in range(TILES):
                    ins = pe.matmul(ps[:, B_COUNT, 0:EXPERTS], ones_b[:], onehot_b[:, j, :],
                                    start=(j == 0), stop=(j == TILES - 1))
                ins.then_inc(s["ranks_done"], 1)

            def experts(k):
                s = ffn[k]

                def turn_x(i):
                    pe.wait_ge(s["tile_loaded"], (i + 1) * 16)
                    pe.wait_ge(s["tile_t_ready"], i)
                    for c in range(KC):
                        ins = pe.transpose(ps[:, B_XT, c * P:(c + 1) * P], x_tile[:, c * P:(c + 1) * P],
                                           ident[:])
                    ins.then_inc(s["tile_turned"], 1)

                def gate_up_of(i, w):
                    pe.wait_ge(s["tile_t_ready"], i + 1)
                    pe.wait_ge(s["hidden_ready"], i)
                    for h, bank in enumerate((B_GATE, B_UP)):
                        for c in range(KC):
                            ins = pe.matmul(ps[:, bank, :], x_t[:, c, :], w(c, h),
                                            start=(c == 0), stop=(c == KC - 1))
                    ins.then_inc(s["gate_up_done"], 1)

                def turn_hidden(i):
                    pe.wait_ge(s["hidden_ready"], i + 1)
                    pe.wait_ge(s["hidden_t_ready"], i)
                    for c in range(FC):
                        ins = pe.transpose(ps[:, B_HT, c * P:(c + 1) * P], hid[:, c * P:(c + 1) * P],
                                           ident[:])
                    ins.then_inc(s["hidden_turned"], 1)

                def down_of(i, w):
                    pe.wait_ge(s["hidden_t_ready"], i + 1)
                    pe.wait_ge(s["y_ready"], i)
                    for c in range(FC):
                        ins = pe.matmul(ps[:, B_Y, 0:DIM], hid_t[:, c, :], w(c),
                                        start=(c == 0), stop=(c == FC - 1))
                    ins.then_inc(s["y_done"], 1)

                def shared_gu(c, h):
                    return w_gu[:, SHARED, c, h * INNER:(h + 1) * INNER]

                def shared_dn(c):
                    return w_dn[:, SHARED, c, :]

                def expert_of(i):
                    return pe.value_load(tile_expert[0:1, bass.ds(i, 1)], min_val=0, max_val=EXPERTS)

                def gu(e):
                    return lambda c, h: w_gu[:, bass.ds(e, 1), c, h * INNER:(h + 1) * INNER]\
                        .rearrange("p a n -> p (a n)")

                def dn(e):
                    return lambda c: w_dn[:, bass.ds(e, 1), c, :].rearrange("p a n -> p (a n)")

                if k == 0:
                    pe.wait_ge(s_wsh, 16 * 3)
                turn_x(0)
                gate_up_of(0, shared_gu)
                turn_x(1)
                turn_hidden(0)

                def shared_tile(i):
                    gate_up_of(i, shared_gu)
                    turn_x(i + 1)
                    down_of(i - 1, shared_dn)
                    turn_hidden(i)

                shared_tile(1)
                with pe.Fori(2, TILES) as i:
                    shared_tile(i)
                pe.wait_ge(s["plan_ready"], 2)
                if k == 0:
                    pe.wait_ge(s_wex, 16 * 2 * EXPERTS)
                n = tile_count(pe)
                with pe.Fori(TILES, n) as i:
                    e, e_before = expert_of(i), expert_of(i - 1)
                    gate_up_of(i, gu(e))
                    turn_x(i + 1)
                    down_of(i - 1, dn(e_before))
                    turn_hidden(i)
                last = tile_count(pe, 1)
                down_of(last, dn(expert_of(last)))

            def qkv():
                pe.wait_ge(s_watt, 16 * 4)
                for j in range(TILES):
                    pe.wait_ge(s_turned, TURNS + j // 2 + 1)
                    if j >= 2:
                        pe.wait_ge(s_qkvc, 3 * (j - 1))
                    for c in range(KC):
                        ins = pe.matmul(ps[:, j % 2, :], xn_t[:, j, c, :], w_qkv[:, c, :],
                                        start=(c == 0), stop=(c == KC - 1))
                    ins.then_inc(s_qkv, 1)

            def set_free(b, unit):
                last = set_before[unit]
                if last is not None:
                    kind, g, h = last
                    pe.wait_ge(s_max if kind == "A" else s_exp, b * UNITS + 2 * g + h + 1)

            def scores(b, kind, g, h):
                st = score_set[kind, g, h]
                set_free(b, (kind, g, h))
                mask = mask_ts if kind == "A" else mask_st
                for m in range(2):
                    bank = ps[:, 2 * st + m, :]
                    pe.matmul(bank.rearrange("p (a c) -> p a c", a=2)[:, :, 0:P], ident_b,
                              mask.unsqueeze(1).to_broadcast([P, 2, P]), start=True, stop=False,
                              skip_group_check=True)
                for part in range(2):
                    for m in range(2):
                        r = SLOT * (2 * h + m)
                        bank = ps[:, 2 * st + m, :]
                        if kind == "A":
                            rows = slice(r, r + ROWS_A)
                            w = qk_t[rows, g % 4, 0, part * P:(part + 1) * P]
                            x = qk_t[rows, g % 4, 1, 0:(part + 1) * P]
                            o = bank[:, 0:P] if part == 0 else bank[:, P:SPAN]
                        else:
                            rows = slice(r, r + ROWS_B)
                            w = qk_t[rows, g % 4, 1, part * P:(part + 1) * P]
                            x = qm_t[rows, g % 2, part * P:SEQ]
                            o = bank[:, 0:SEQ] if part == 0 else bank[:, SEQ:SPAN]
                        ins = pe.matmul(o, w, x, start=False, stop=True, skip_group_check=True)
                ins.then_inc(s_ascore if kind == "A" else s_bscore, 1)

            def attention(b):
                def misc_free(use):
                    at = misc_order.index(use)
                    if at > 0:
                        kind, g = misc_order[at - 1]
                        pe.wait_ge({"QK": s_filc, "QM": s_qmc, "O": s_otc}[kind], b * GROUPS + g + 1)

                def turn_qk(g):
                    misc_free(("QK", g))
                    for n in range(2):
                        for i in range(HALVES):
                            src = q_pad[:, i, 4 * g:4 * g + 4].rearrange("p n s -> p (n s)") if n == 0 \
                                else k_pad[:, i, 2 * g:2 * g + 2].rearrange("p k u s -> p (k u s)")
                            ins = pe.transpose(ps[:, B_MISC, (2 * n + i) * P:(2 * n + i + 1) * P], src,
                                               ident[:])
                    ins.then_inc(s_fill, 1)

                pe.wait_ge(s_pad, (b + 1) * 3 * HALVES)
                turn_qk(0)
                pe.wait_ge(s_vnow, (b + 1) * HALVES)
                for u in range(GROUPS + LAG_O):
                    if u < GROUPS:
                        pe.wait_ge(s_filc, b * GROUPS + u + 1)
                        scores(b, "A", u, 0)
                        scores(b, "A", u, 1)
                    if u + 1 < GROUPS:
                        turn_qk(u + 1)
                    g = u - LAG_B
                    if 0 <= g < GROUPS:
                        pe.wait_ge(s_neg, b * GROUPS + g + 1)
                        misc_free(("QM", g))
                        for i in range(HALVES):
                            ins = pe.transpose(ps[:, B_MISC, i * P:(i + 1) * P],
                                               q_pad[:, i, 4 * g:4 * g + 4].rearrange("p n s -> p (n s)"),
                                               ident[:])
                        ins.then_inc(s_qm, 1)
                        pe.wait_ge(s_qmc, b * GROUPS + g + 1)
                        scores(b, "B", g, 0)
                        scores(b, "B", g, 1)
                    g = u - LAG_PV
                    if 0 <= g < GROUPS:
                        pe.wait_ge(s_exp, b * UNITS + 2 * g + 2)
                        if g > 0:
                            pe.wait_ge(s_oc, b * GROUPS + g)
                        for i in range(HALVES):
                            for r in range(4):
                                pr = probs[:, (2 * g + r // 2) % 4, r % 2, :]
                                ins = pe.matmul(ps[SLOT * r:SLOT * (r + 1), B_O, i * P:SEQ],
                                                v_now[:, i, g, :], pr[:, 0:SEQ] if i == 0 else pr[:, SEQ:SPAN],
                                                start=(i == 0), stop=(i == 1), skip_group_check=True)
                        ins.then_inc(s_pv, 1)
                    g = u - LAG_O
                    if 0 <= g < GROUPS:
                        pe.wait_ge(s_oc, b * GROUPS + g + 1)
                        misc_free(("O", g))
                        for i in range(HALVES):
                            ins = pe.transpose(ps[:, B_MISC, i * P:(i + 1) * P], o_t[:, i * P:(i + 1) * P],
                                               ident[:])
                        ins.then_inc(s_ot, 1)

            def project():
                pe.wait_ge(s_wo, 1)
                for j in range(TILES):
                    pe.wait_ge(s_turned, 2 * TURNS + j // 2 + 1)
                    if j >= 2:
                        pe.wait_ge(s_res, TILES + j - 1)
                    for c in range(KC):
                        ins = pe.matmul(ps[:, j % 2, 0:DIM], xn_t[:, j, c, :], w_o[:, c, :],
                                        start=(c == 0), stop=(c == KC - 1))
                    ins.then_inc(s_proj, 1)

            pe.wait_ge(s_small, 16 * N_SMALL)
            pe.wait_ge(s_const, N_CONST)
            pe.wait_ge(s_tables, 1)
            turn(0, xn, ln_ready(0))
            route(0)
            experts(0)
            turn(1, xn, ln_ready(1))
            qkv()
            with pe.Fori(0, BATCH) as b:
                attention(b)
            turn(2, attn, lambda f: pe.wait_ge(s_attn, BATCH))
            project()
            turn(3, xn, ln_ready(2))
            route(1)
            experts(1)


_INS = ["L0_attn_x", "L0_attn_Wq", "L0_attn_Wk", "L0_attn_Wv", "L0_attn_Wo", "L0_attn_lam_q1",
        "L0_attn_lam_k1", "L0_attn_lam_q2", "L0_attn_lam_k2", "L0_attn_g", "L0_ffn_router_w",
        "L0_ffn_gate_up_proj", "L0_ffn_down_proj", "L0_ffn_shared_gate_w", "L0_ffn_shared_up_w",
        "L0_ffn_shared_down_w"]


def _constants():
    import numpy as np
    at = np.arange(P)
    hidden = np.float32(-3e38)
    tables = np.stack([np.eye(P), np.where(at[None, :] > at[:, None], hidden, 0.0),
                       np.where(at[:, None] > at[None, :], hidden, 0.0),
                       at[:, None] < at[None, :]], axis=1).astype(np.float32)
    freq = (1.0 / 10000.0 ** (np.arange(0, HD, 2, dtype=np.float32) / HD)).astype(np.float32)
    angle = np.arange(SEQ, dtype=np.float32)[:, None] * freq[None, :]
    cos, sin = np.cos(angle), np.sin(angle)
    rope = np.stack([np.concatenate([cos, cos], 1), np.concatenate([sin, -sin], 1)], axis=1)
    return {"ident": np.eye(P, dtype=np.float32), "tables": tables, "rope": rope.astype(np.float32)}


def kernel(**inputs):
    import numpy as _np
    import concourse.bacc as _bacc
    from concourse import mybir as _mybir
    from concourse.bass_utils import run_bass_kernel_spmd as _run

    nc = _bacc.Bacc("TRN2", target_bir_lowering=False, num_devices=1)
    given = {name: _np.asarray(inputs[name]) for name in _INS}
    given["L0_ffn_router_w"] = given["L0_ffn_router_w"].T
    given.update(_constants())
    arrays, args = {}, []
    for name, a in given.items():
        a = _np.ascontiguousarray(a)
        arrays[f"in_{name}_dram"] = a
        args.append(nc.dram_tensor(f"in_{name}_dram", a.shape, _mybir.dt.from_np(a.dtype), kind="ExternalInput").ap())
    args.append(nc.dram_tensor("out_0_dram", (BATCH, SEQ, DIM), F32, kind="ExternalOutput").ap())
    bass_macaron(nc, *args)
    r = _run(nc, [arrays], core_ids=[0])
    return r.results[0]["out_0_dram"]
```

```python
from contextlib import ExitStack
import math

import concourse.bass as bass
from concourse import mybir

ALU = mybir.AluOpType
ACT = mybir.ActivationFunctionType
AX_X = mybir.AxisListType.X
F32 = mybir.dt.float32
F32R = mybir.dt.float32r
BF16 = mybir.dt.bfloat16
I32 = mybir.dt.int32
U32 = mybir.dt.uint32

P = 128
BATCH, SEQ, DIM = 4, 256, 256
TILES = BATCH * SEQ // P
HALVES = SEQ // P
KC = DIM // P
EXPERTS, INNER = 8, 512
SHARED = EXPERTS
FC = INNER // P
ROUTED_MAX = TILES + EXPERTS - 1
ROUTED_SLOTS = ROUTED_MAX + 1
HEADS, KV_HEADS = 16, 8
QSUB, KSUB = 2 * HEADS, 2 * KV_HEADS
HD = DIM // HEADS // 2
VD = 2 * HD
SLOT = 32
GROUPS = QSUB // 4
SPAN = 3 * P
LN_EPS, RMS_EPS = 1e-5, 1e-6
LAMBDA_INIT = 0.8 - 0.6 * math.exp(-0.3 * 12)
ALL_GROUPS = BATCH * GROUPS
LAG_B, LAG_PV, LAG_DIF, LAG_SUM, AHEAD = 2, 3, 4, 5, 3
FIRST = 5
RING, RING_T = 8, 4
SET_OF = {("A", 0): 0, ("A", 1): 1, ("B", 0): 0, ("B", 1): 2}
ROWS_A, ROWS_B = 3 * HD, 3 * HD + 2
TURNS = TILES // 2
LESS = (0, 1, TILES, TILES + 1)
N_CONST = 16
N_SMALL, N_LATE = 3, 5 + P // VD
WARM_UP = 4
QK_LIMIT = 2.0 ** 60
N_QKV = DIM + 2 * KV_HEADS * VD


def bass_macaron(nc, x_in, wq, wk, wv, wo, lam_q1, lam_k1, lam_q2, lam_k2, g, router_t, gate_up,
                 down, sh_gate, sh_up, sh_down, ident_in, tables_in, rope_in, out):
    x_rows = x_in.rearrange("b (i p) d -> (b i p) d", p=P)
    out_rows = out.rearrange("b (i p) d -> (b i p) d", p=P)
    with ExitStack() as ctx:
        def sb(name, shape, dt=F32):
            return ctx.enter_context(nc.sbuf_tensor(name, shape, dt))

        def sem(name):
            return ctx.enter_context(nc.semaphore(name))

        w_gu = sb("w_gu", [P, EXPERTS + 1, KC, 2 * INNER])
        w_dn = sb("w_dn", [P, EXPERTS + 1, FC, DIM])
        w_qkv = sb("w_qkv", [P, KC, N_QKV])
        w_o = sb("w_o", [P, KC, DIM])
        w_rt = sb("w_rt", [P, KC, EXPERTS])
        ident = sb("ident", [P, P])
        tables = sb("tables", [P, 4, P], BF16)
        ident_b, mask_ts, mask_st, before = (tables[:, n, :] for n in range(4))
        ones_b = sb("ones_b", [P, P], BF16)
        rope = sb("rope", [P, HALVES, 2, HD])
        iota8 = sb("iota8", [P, EXPERTS])
        steps = sb("steps", [P, ROUTED_MAX + 1])
        steps_128 = sb("steps_128", [P, TILES])
        ones8 = sb("ones8", [P, EXPERTS])
        minus_half = sb("minus_half", [P, 1])
        lam_in = sb("lam_in", [P, 4, HD])
        lam_pr = sb("lam_pr", [P, 2, HD])
        lam_s = sb("lam_s", [P, 2])
        lam_e = sb("lam_e", [P, 2])
        neg_lam = sb("neg_lam", [P, 1])
        g_col = sb("g_col", [P, 1])
        x_res = sb("x_res", [P, TILES, DIM])
        xn = sb("xn", [P, TILES, DIM])
        moved = sb("moved", [P, TILES, DIM])
        stats = sb("stats", [P, TILES, 6])
        mean_var = sb("mean_var", [P, TILES, 2])
        var_eps = sb("var_eps", [P, TILES])
        rstd = sb("rstd", [P, TILES])
        xn_t = sb("xn_t", [P, TILES, KC, P])
        top = sb("top", [P, TILES])
        score = sb("score", [P, TILES])
        is_top = sb("is_top", [P, TILES, EXPERTS])
        key = sb("key", [P, TILES, EXPERTS])
        pick = sb("pick", [P, TILES])
        onehot = sb("onehot", [P, TILES, EXPERTS])
        onehot_b = sb("onehot_b", [P, TILES, EXPERTS], BF16)
        count = sb("count", [P, EXPERTS])
        over = sb("over", [P, EXPERTS, TILES])
        e_tiles = sb("e_tiles", [P, EXPERTS])
        e_end = sb("e_end", [P, EXPERTS])
        e_start = sb("e_start", [P, EXPERTS])
        pos = sb("pos", [P, TILES])
        pos_u = sb("pos_u", [P, TILES], U32)
        t_exp = sb("t_exp", [P, ROUTED_MAX + 1])
        tile_expert = sb("tile_expert", [P, TILES + ROUTED_SLOTS], I32)
        n_base = sb("n_base", [P, len(LESS)])
        n_tiles = sb("n_tiles", [P, len(LESS)], I32)
        x_tile = sb("x_tile", [P, DIM])
        x_t = sb("x_t", [P, KC, P])
        work = sb("work", [P, 4, INNER])
        act_g, hid = work[:, 0, :], work[:, 1, :]
        hid_t = work[:, 2, :].rearrange("p (c t) -> p c t", t=P)
        y_tile = sb("y_tile", [P, DIM])
        past = work[:, 3, 0:P].rearrange("p (t e) -> p t e", e=EXPERTS)
        place = work[:, 3, P:P + TILES * EXPERTS].rearrange("p (t e) -> p t e", e=EXPERTS)
        place2 = work[:, 3, 2 * P:2 * P + TILES * EXPERTS].rearrange("p (t e) -> p t e", e=EXPERTS)
        zero_row = y_tile
        q_all = xn[:].rearrange("p t (n d) -> p t n d", d=HD)
        k_all = xn_t[:].rearrange("p t c m -> p t (c m)")
        v_all = sb("v_all", [P, TILES, KV_HEADS * VD])
        v_pad = sb("v_pad", [P, RING, HALVES, SLOT])
        probs = sb("probs", [P, 4, 2, SPAN])
        qk_in = work[:, 0:2, 0:SPAN].rearrange("p a (n d) -> p a n d", d=HD)
        rot_cos = probs[:, 0:2, 0, :].rearrange("p a (n d) -> p a n d", d=HD)
        rot_sin = probs[:, 0:2, 1, :].rearrange("p a (n d) -> p a n d", d=HD)
        q_pad = sb("q_pad", [P, RING, HALVES, 4, SLOT], F32R)
        k_pad = sb("k_pad", [P, RING_T, HALVES, 4, SLOT], F32R)
        ident_r = sb("ident_r", [P, P], F32R)
        qk_t = sb("qk_t", [P, RING_T, 2, SEQ], F32R)
        qm_t = sb("qm_t", [P, 2, SEQ], F32R)
        blk_max = sb("blk_max", [P, 4 * RING_T, 4])
        neg_max = sb("neg_max", [P, HALVES, 4 * RING_T])
        o_t = x_t[:].rearrange("p c t -> p (c t)")
        o_inv = sb("o_inv", [P, HALVES, 4])
        o_sc = sb("o_sc", [P, 2, HALVES, 4, VD])
        o_sq = sb("o_sq", [P, 2, HALVES, 2, VD])
        o_ms = sb("o_ms", [P, TILES * HEADS])
        o_me = sb("o_me", [P, TILES * HEADS])
        o_rs = sb("o_rs", [P, TILES * HEADS])
        attn = moved

        ps = ctx.enter_context(nc.psum_tensor("ps", [P, 8, 512], F32))
        B_GATE, B_UP, B_HT, B_XT, B_Y, B_LOGIT, B_RANK, B_COUNT = range(8)
        B_TURN = (B_HT, B_XT)
        B_MISC, B_O = 6, 7

        slots = nc.dram_tensor("slots", (ROUTED_SLOTS * P, DIM), F32).ap()

        s_x = [sem(f"x_loaded_{f}") for f in range(TURNS)]
        s_gathered = [sem(f"gathered_{j}") for j in range(TILES)]
        s_small = sem("small_loaded")
        s_late = sem("attention_vectors_loaded")
        s_wsh = sem("shared_weights_loaded")
        s_wex = sem("expert_weights_loaded")
        s_watt = sem("attention_weights_loaded")
        s_tables = sem("tables_ready")
        s_const = sem("pool_constants")
        s_zero = sem("slots_zeroed")
        s_lam = sem("lambda_steps")
        s_lame = sem("lambda_exps")
        s_dve = sem("dve_chain")
        s_pool = sem("pool_chain")
        s_stat = sem("ln_stats")
        s_mv = sem("ln_mean_var")
        s_rstd = sem("ln_rstd")
        s_xn = sem("xn_ready")
        s_turn = sem("tiles_turned")
        s_turned = sem("turned_tiles_copied")
        s_res = sem("residual_updated")
        s_out = sem("out_stored")

        s_qkv = sem("qkv_done")
        s_clamp = sem("qk_clamped")
        s_vall = sem("v_copied")
        s_cos = sem("cos_parts")
        s_sin = sem("sin_parts")
        s_rot = sem("qk_rotated")
        s_hi = sem("qk_high_parts")
        s_pad = sem("qk_split")
        s_fill = sem("qk_turned")
        s_filc = sem("qk_turned_copied")
        s_ascore = sem("row_scores_done")
        s_max = sem("row_max_done")
        s_row = sem("neg_row_max_ready")
        s_neghi = sem("neg_max_high_part")
        s_neg = sem("neg_max_ready")
        s_qm = sem("q_max_turned")
        s_qmc = sem("q_max_copied")
        s_bscore = sem("column_scores_done")
        s_exp = sem("exp_done")
        s_pv = sem("pv_done")
        s_oc = sem("o_copied")
        s_ot = sem("o_turned")
        s_inv = sem("o_inverses")
        s_scaled = sem("o_scaled")
        s_dif = sem("o_differences")
        s_sq = sem("o_squares")
        s_ms = sem("o_square_sums")
        s_mean = sem("o_mean_squares")
        s_root = sem("o_roots")
        s_attn = sem("attn_ready")
        s_passed = sem("pool_waits_passed")
        s_wo = sem("wo_scaled")
        s_proj = sem("projected")

        block = ctx.enter_context(nc.Block())
        names = ("logits_done", "top_ready", "score_ready", "onehot_ready", "ranks_done",
                 "scaled_ready", "pos_ready", "plan_ready", "scattered", "tile_loaded", "tile_turned",
                 "tile_t_ready", "gate_up_done", "silu_done", "hidden_ready", "hidden_turned",
                 "hidden_t_ready", "y_done", "y_ready", "y_stored")
        ffn = [{n: sem(f"{n}_{k}") for n in names} for k in range(2)]

        class Chain:

            def __init__(self, eng, s, base=0, passed=None):
                self.eng, self.s, self.base, self.passed, self.n = eng, s, base, passed, 0

            def step(self, ins):
                self.n += 1
                ins.then_inc(self.s, 1)
                self.eng.wait_ge(self.s, self.base + self.n)
                if self.passed is not None:
                    self.eng.sem_inc(self.passed, 1)

        def one(t, j):
            return t[:, bass.ds(j, 1), :].rearrange("p a d -> p (a d)")

        def rows_of(t, b, g, cols):
            return t[:, bass.ds((b + g // GROUPS) * HALVES, HALVES), cols]

        def attention_steps(eng, step, before_loop=None):
            for u in range(FIRST):
                step(0, u)
            if before_loop is not None:
                before_loop()
            with eng.Fori(0, BATCH - 1) as b:
                for u in range(FIRST, FIRST + GROUPS):
                    step(b, u)
            for u in range(FIRST + (BATCH - 1) * GROUPS, ALL_GROUPS + LAG_SUM):
                step(0, u)

        def tile_count(eng, less=0):
            at = LESS.index(less)
            return eng.value_load(n_tiles[0:1, at:at + 1], min_val=2 * TILES - less,
                                  max_val=TILES + ROUTED_MAX - less)

        @block.sync
        def _(sp):
            sp.dma_start(ident[:], ident_in).then_inc(s_small, 16)
            for f in range(TURNS):
                sp.dma_start(x_res[:, 2 * f:2 * f + 2, :], x_rows[2 * f * P:2 * (f + 1) * P, :]
                             .rearrange("(j p) d -> p j d", p=P)).then_inc(s_x[f], 16)
            sp.dma_start(w_rt[:], router_t.rearrange("(c p) e -> p c e", p=P)).then_inc(s_small, 16)
            sp.dma_start(work[:, 0, :], tables_in.rearrange("p n m -> p (n m)")).then_inc(s_small, 16)
            sp.wait_ge(s_const, 1)
            sp.dma_start(slots.rearrange("(i p) d -> p i d", p=P),
                         zero_row[:].unsqueeze(1).to_broadcast([P, ROUTED_SLOTS, DIM]))\
                .then_inc(s_zero, 16)
            for k in range(2):
                s = ffn[k]
                sp.wait_ge(s["scattered"], 16 * TILES)
                sp.wait_ge(s["plan_ready"], 2)
                routed, last = tile_count(sp, TILES), tile_count(sp, TILES + 1)
                sp.dma_start(x_tile[:], slots[0:P, :]).then_inc(s["tile_loaded"], 16)
                sp.wait_ge(s["tile_turned"], 1)
                sp.dma_start(x_tile[:], slots[P:2 * P, :]).then_inc(s["tile_loaded"], 16)
                with sp.Fori(1, routed) as r:
                    sp.wait_ge(s["tile_turned"], r + 1)
                    sp.dma_start(x_tile[:], slots[bass.ds((r + 1) * P, P), :])\
                        .then_inc(s["tile_loaded"], 16)
                    sp.wait_ge(s["y_ready"], r + TILES)
                    sp.dma_start(slots[bass.ds((r - 1) * P, P), :], y_tile[:])\
                        .then_inc(s["y_stored"], 16)
                sp.wait_ge(s["y_ready"], routed + TILES)
                sp.dma_start(slots[bass.ds(last * P, P), :], y_tile[:])\
                    .then_inc(s["y_stored"], 16)
            with sp.Fori(0, TILES) as j:
                sp.wait_ge(s_res, 2 * TILES + j + 1)
                sp.dma_start(out_rows[bass.ds(j * P, P), :], one(x_res, j)).then_inc(s_out, 16)
            sp.wait_ge(s_out, 16 * TILES)

        @block.gpsimd
        def _(pool):
            chain = Chain(pool, s_pool)
            pool.memset(zero_row[:], 0.0).then_inc(s_const, 1)
            pool.memset(ones_b[:], 1.0).then_inc(s_const, 1)
            pool.memset(ones8[:], 1.0).then_inc(s_const, 1)
            pool.memset(minus_half[:], -0.5).then_inc(s_const, 1)
            pool.iota(iota8[:], [[1, EXPERTS]], base=-EXPERTS, channel_multiplier=0,
                      allow_small_or_imprecise_dtypes=True).then_inc(s_const, 1)
            pool.iota(steps[:], [[1, ROUTED_MAX + 1]], base=0, channel_multiplier=0,
                      allow_small_or_imprecise_dtypes=True).then_inc(s_const, 1)
            pool.iota(steps_128[:], [[P, TILES]], base=0, channel_multiplier=0,
                      allow_small_or_imprecise_dtypes=True).then_inc(s_const, 1)
            pool.memset(blk_max[:, :, 0:1], 3e38).then_inc(s_const, 1)
            for at, less in enumerate(LESS):
                pool.memset(n_base[:, at:at + 1], float(TILES - less)).then_inc(s_const, 1)
            pool.memset(k_pad[:].bitcast(F32), 1.0).then_inc(s_const, 1)
            pool.memset(q_pad[:].bitcast(F32), 0.0).then_inc(s_const, 1)
            pool.memset(v_pad[:], 0.0).then_inc(s_const, 1)
            pool.wait_ge(s_const, N_CONST - 1)
            pool.memset(v_pad[:, :, :, VD:VD + 1], 1.0).then_inc(s_const, 1)
            pool.wait_ge(s_const, N_CONST)

            def loop_wait(s, value):
                pool.wait_ge(s, value)
                pool.sem_inc(s_passed, 1)

            def rstds(n):
                for j in range(TILES):
                    pool.wait_ge(s_mv, n * TILES + j + 1)
                    chain.step(pool.tensor_scalar(var_eps[:, j:j + 1], mean_var[:, j, 1:2], LN_EPS, None,
                                                  ALU.add))
                    pool.tensor_tensor(rstd[:, j:j + 1], var_eps[:, j:j + 1], minus_half[:], ALU.pow)\
                        .then_inc(s_rstd, 1)

            def route(k):
                s = ffn[k]
                pool.wait_ge(s["pos_ready"], 1)
                pool.wait_ge(s["scaled_ready"], TILES)
                if k == 0:
                    pool.wait_ge(s_zero, 16)
                for j in range(TILES):
                    pool.indirect_dma_start(
                        out=slots, out_offset=bass.IndirectOffsetOnAxis(ap=pos_u[:, j:j + 1], axis=0),
                        in_=moved[:, j, :], in_offset=None).then_inc(s["scattered"], 16)
                pool.wait_ge(s["plan_ready"], 2)
                routed = tile_count(pool, TILES)
                pool.wait_ge(s["scattered"], 16 * TILES)
                loop_wait(s["y_stored"], routed * 16)
                for j in range(TILES):
                    pool.indirect_dma_start(
                        out=moved[:, j, :], out_offset=None, in_=slots,
                        in_offset=bass.IndirectOffsetOnAxis(ap=pos_u[:, j:j + 1], axis=0))\
                        .then_inc(s_gathered[j], 16)

            def rotary():
                pool.wait_ge(s_late, 16 * N_LATE)
                low, high = slice(0, HD // 2), slice(HD // 2, HD)
                for j in range(TILES):
                    sin = rope[:, j % HALVES, 1:2, :]
                    pool.wait_ge(s_clamp, j + 1)
                    if j >= 2:
                        pool.wait_ge(s_rot, 2 * (j - 1))
                    for to, frm in ((low, high), (high, low)):
                        pool.tensor_tensor(rot_sin[:, j % 2, :, to], qk_in[:, j % 2, :, frm],
                                           sin[:, :, to].to_broadcast([P, QSUB + KSUB, HD // 2]),
                                           ALU.mult).then_inc(s_sin, 1)

            def split(b, g):
                r = g % RING
                qd = slice(4 * (g % GROUPS) * HD, (4 * (g % GROUPS) + 4) * HD)
                q = rows_of(xn, b, g, qd).rearrange("p i (n d) -> p i n d", d=HD)
                k = rows_of(k_all, b, g, qd).rearrange("p i (n d) -> p i n d", d=HD)
                if g >= RING:
                    loop_wait(s_pv, b * GROUPS + g - RING + 1)
                vd = slice(g % GROUPS * VD, (g % GROUPS + 1) * VD)
                pool.tensor_copy(v_pad[:, r, :, 0:VD], rows_of(v_all, b, g, vd)).then_inc(s_hi, 1)
                for at in (0, 2):
                    pool.tensor_copy(q_pad[:, r, :, :, at * HD:(at + 1) * HD], q).then_inc(s_hi, 1)
                for at in (0, 1):
                    pool.tensor_copy(k_pad[:, g % RING_T, :, :, at * HD:(at + 1) * HD], k).then_inc(s_hi, 1)
                loop_wait(s_hi, (b * GROUPS + g + 1) * 5)
                pool.tensor_tensor(q_pad[:, r, :, :, HD:2 * HD], q,
                                   q_pad[:, r, :, :, 0:HD].bitcast(F32), ALU.subtract).then_inc(s_pad, 1)
                pool.tensor_tensor(k_pad[:, g % RING_T, :, :, 2 * HD:3 * HD], k,
                                   k_pad[:, g % RING_T, :, :, 0:HD].bitcast(F32), ALU.subtract).then_inc(s_pad, 1)

            def split_max(b, g):
                r, m = g % RING, slice(4 * (g % RING_T), 4 * (g % RING_T) + 4)
                loop_wait(s_row, b * GROUPS + g + 1)
                pool.tensor_copy(q_pad[:, r, :, :, ROWS_A], neg_max[:, :, m]).then_inc(s_neghi, 1)
                pool.wait_ge(s_neghi, b * GROUPS + g + 1)
                pool.tensor_tensor(q_pad[:, r, :, :, ROWS_A + 1], neg_max[:, :, m],
                                   q_pad[:, r, :, :, ROWS_A].bitcast(F32), ALU.subtract)\
                    .then_inc(s_neg, 1)

            def difference(b, g):
                hd = slice(2 * (g % GROUPS) * VD, (2 * (g % GROUPS) + 2) * VD)
                o = rows_of(attn, b, g, hd).rearrange("p i (n d) -> p i n d", d=VD)
                pair = o_sc[:, g % 2].rearrange("p i (n two) d -> p i n two d", two=2)
                loop_wait(s_scaled, b * GROUPS + g + 1)
                pool.tensor_tensor(o, pair[:, :, :, 0, :], pair[:, :, :, 1, :], ALU.add)\
                    .then_inc(s_dif, 1)
                loop_wait(s_dif, b * GROUPS + g + 1)
                pool.tensor_tensor(o_sq[:, g % 2], o, o, ALU.mult).then_inc(s_sq, 1)

            def attention(b, u):
                if 0 <= u - LAG_DIF < ALL_GROUPS:
                    difference(b, u - LAG_DIF)
                if u + AHEAD < ALL_GROUPS:
                    split(b, u + AHEAD)
                if u < ALL_GROUPS:
                    split_max(b, u)

            rstds(0)
            route(0)
            rstds(1)
            rotary()
            pool.wait_ge(s_rot, 2 * TILES)
            for g in range(AHEAD):
                split(0, g)
            attention_steps(pool, attention)
            rstds(2)
            route(1)

        @block.vector
        def _(dve):
            chain = Chain(dve, s_dve)

            def layernorm(n, arrive):
                for u in range(TILES + 4):
                    if u < TILES:
                        arrive(u)
                    j = u - 1
                    if 0 <= j < TILES:
                        if n > 0:
                            dve.wait_ge(s_res, n * TILES + j + 1 - TILES)
                        dve.bn_stats(stats[:, j, :], x_res[:, j, :]).then_inc(s_stat, 1)
                    j = u - 2
                    if 0 <= j < TILES:
                        dve.wait_ge(s_stat, n * TILES + j + 1)
                        dve.bn_aggr(mean_var[:, j, :], stats[:, j, :]).then_inc(s_mv, 1)
                    j = u - 4
                    if 0 <= j < TILES:
                        dve.wait_ge(s_rstd, n * TILES + j + 1)
                        dve.tensor_scalar(xn[:, j, :], x_res[:, j, :], mean_var[:, j, 0:1],
                                          rstd[:, j:j + 1], ALU.subtract, ALU.mult).then_inc(s_xn, 1)

            def loaded(j):
                if j % 2 == 0:
                    dve.wait_ge(s_x[j // 2], 16)

            def add_routed(k):
                def arrive(j):
                    dve.wait_ge(s_gathered[j], 16 * (k + 1))
                    dve.scalar_tensor_tensor(x_res[:, j, :], moved[:, j, :], 0.5, x_res[:, j, :],
                                             ALU.mult, ALU.add).then_inc(s_res, 1)
                return arrive

            def add_projected(j):
                dve.wait_ge(s_proj, j + 1)
                dve.tensor_tensor(x_res[:, j, :], x_res[:, j, :], ps[:, j % 2, 0:DIM], ALU.add)\
                    .then_inc(s_res, 1)

            def plan(k):
                s = ffn[k]
                full = [P, TILES, EXPERTS]
                logits = ps[:, B_LOGIT, 0:TILES * EXPERTS].rearrange("p (t e) -> p t e", e=EXPERTS)
                rank = ps[:, B_RANK, 0:TILES * EXPERTS].rearrange("p (t e) -> p t e", e=EXPERTS)
                dve.wait_ge(s["logits_done"], 1)
                dve.tensor_reduce(top[:], logits, AX_X, ALU.max).then_inc(s["top_ready"], 1)
                dve.wait_ge(s["top_ready"], 1)
                chain.step(dve.tensor_tensor(is_top[:], logits, top[:].unsqueeze(2).to_broadcast(full),
                                             ALU.is_equal))
                chain.step(dve.scalar_tensor_tensor(key[:], is_top[:], -float(EXPERTS),
                                                    iota8[:].unsqueeze(1).to_broadcast(full),
                                                    ALU.mult, ALU.add))
                chain.step(dve.tensor_reduce(pick[:], key[:], AX_X, ALU.min))
                dve.tensor_tensor(onehot_b[:], key[:], pick[:].unsqueeze(2).to_broadcast(full),
                                  ALU.is_equal).then_inc(s["onehot_ready"], 1)
                dve.wait_ge(s["score_ready"], 1)
                for j in range(TILES):
                    dve.tensor_scalar(moved[:, j, :], xn[:, j, :], score[:, j:j + 1], None, ALU.mult)\
                        .then_inc(s["scaled_ready"], 1)
                dve.wait_ge(s["ranks_done"], 1)
                chain.step(dve.tensor_copy(count[:], ps[:, B_COUNT, 0:EXPERTS]))
                chain.step(dve.tensor_tensor(over[:], count[:].unsqueeze(2).to_broadcast([P, EXPERTS, TILES]),
                                             steps_128[:].unsqueeze(1).to_broadcast([P, EXPERTS, TILES]),
                                             ALU.is_gt))
                chain.step(dve.tensor_reduce(e_tiles[:], over[:], AX_X, ALU.add))
                chain.step(dve.tensor_tensor_scan(e_end[:], ones8[:], e_tiles[:], 0.0, ALU.mult, ALU.add))
                chain.step(dve.tensor_tensor(e_start[:], e_end[:], e_tiles[:], ALU.subtract))
                chain.step(dve.scalar_tensor_tensor(place, e_start[:].unsqueeze(1).to_broadcast(full),
                                                    float(P), rank, ALU.mult, ALU.add))
                chain.step(dve.tensor_tensor(place2, place, onehot_b[:], ALU.mult))
                chain.step(dve.tensor_reduce(pos[:], place2, AX_X, ALU.add))
                dve.tensor_copy(pos_u[:], pos[:]).then_inc(s["pos_ready"], 1)
                wide = [P, ROUTED_MAX + 1, EXPERTS]
                chain.step(dve.tensor_tensor(past, e_end[:].unsqueeze(1).to_broadcast(wide),
                                             steps[:].unsqueeze(2).to_broadcast(wide), ALU.is_le))
                chain.step(dve.tensor_reduce(t_exp[:], past, AX_X, ALU.add))
                dve.tensor_scalar(tile_expert[:, TILES:], t_exp[:], float(EXPERTS - 1), None,
                                  ALU.min).then_inc(s["plan_ready"], 1)
                dve.tensor_scalar(n_tiles[:], n_base[:], e_end[:, EXPERTS - 1:EXPERTS], None,
                                  ALU.add).then_inc(s["plan_ready"], 1)

            def experts(k):
                s = ffn[k]

                def shared_x(i, x):
                    dve.wait_ge(s["gate_up_done"], i)
                    dve.tensor_copy(x_t[:].rearrange("p c t -> p (c t)"), x).then_inc(s["tile_t_ready"], 1)

                def turned(i):
                    dve.wait_ge(s["tile_turned"], i - (TILES - 1))
                    dve.wait_ge(s["gate_up_done"], i)
                    dve.tensor_copy(x_t[:], ps[:, B_XT, 0:DIM].rearrange("p (c t) -> p c t", t=P))\
                        .then_inc(s["tile_t_ready"], 1)

                def hidden(i):
                    dve.wait_ge(s["silu_done"], i + 1)
                    dve.wait_ge(s["hidden_turned"], i)
                    dve.tensor_tensor(hid, act_g, ps[:, B_UP, :], ALU.mult)\
                        .then_inc(s["hidden_ready"], 1)

                def add_shared(i, x):
                    dve.wait_ge(s["y_done"], i + 1)
                    dve.scalar_tensor_tensor(x, ps[:, B_Y, 0:DIM], 0.5, x, ALU.mult, ALU.add)\
                        .then_inc(s["y_ready"], 1)

                def copy_routed(i):
                    dve.wait_ge(s["y_done"], i + 1)
                    dve.tensor_copy(y_tile[:], ps[:, B_Y, 0:DIM]).then_inc(s["y_ready"], 1)

                dve.wait_ge(s_turned, (1, 4)[k] * TURNS)
                xs = xn_t[:].rearrange("p t c m -> p t (c m)")
                dve.tensor_copy(x_t[:].rearrange("p c t -> p (c t)"), xs[:, 0, :])\
                    .then_inc(s["tile_t_ready"], 1)
                shared_x(1, xs[:, 1, :])
                hidden(0)
                with dve.Fori(1, TILES - 1) as i:
                    shared_x(i + 1, one(xs, i + 1))
                    hidden(i)
                    add_shared(i - 1, one(x_res, i - 1))
                turned(TILES)
                hidden(TILES - 1)
                add_shared(TILES - 2, x_res[:, TILES - 2, :])
                turned(TILES + 1)
                hidden(TILES)
                add_shared(TILES - 1, x_res[:, TILES - 1, :])
                n = tile_count(dve)
                turned(TILES + 2)
                hidden(TILES + 1)
                copy_routed(TILES)
                with dve.Fori(TILES + 2, n) as i:
                    turned(i + 1)
                    hidden(i)
                    dve.wait_ge(s["y_stored"], (i - (TILES + 1)) * 16)
                    copy_routed(i - 1)
                dve.wait_ge(s["y_stored"], tile_count(dve, TILES + 1) * 16)
                dve.wait_ge(s["y_done"], n)
                dve.tensor_copy(y_tile[:], ps[:, B_Y, 0:DIM]).then_inc(s["y_ready"], 1)

            def rotary():
                def add(j):
                    dve.wait_ge(s_cos, j + 1)
                    dve.wait_ge(s_sin, 2 * (j + 1))
                    dve.tensor_tensor(q_all[:, j], rot_cos[:, j % 2, 0:QSUB], rot_sin[:, j % 2, 0:QSUB],
                                      ALU.add).then_inc(s_rot, 1)
                    twice = [P, KSUB, 2, HD]
                    dve.tensor_tensor(k_all[:, j].rearrange("p (n u d) -> p n u d", u=2, d=HD),
                                      rot_cos[:, j % 2, QSUB:].unsqueeze(2).to_broadcast(twice),
                                      rot_sin[:, j % 2, QSUB:].unsqueeze(2).to_broadcast(twice),
                                      ALU.add).then_inc(s_rot, 1)

                for j in range(TILES):
                    dve.wait_ge(s_qkv, j + 1)
                    if j >= 2:
                        dve.wait_ge(s_sin, 2 * (j - 1))
                    dve.tensor_scalar(qk_in[:, j % 2].rearrange("p n d -> p (n d)"), ps[:, j % 2, 0:SPAN],
                                      QK_LIMIT, -QK_LIMIT, ALU.min, ALU.max).then_inc(s_clamp, 1)
                    if j >= 1:
                        add(j - 1)
                    dve.wait_ge(s_clamp, j + 1)
                    dve.tensor_tensor(rot_cos[:, j % 2], qk_in[:, j % 2],
                                      rope[:, j % HALVES, 0:1, :].to_broadcast([P, QSUB + KSUB, HD]),
                                      ALU.mult).then_inc(s_cos, 1)
                add(TILES - 1)

            def row_max(b, g):
                m = 4 * (g % RING_T)
                for h in range(2):
                    st = SET_OF["A", h]
                    dve.wait_ge(s_ascore, (b * GROUPS + g) * 2 + h + 1)
                    dve.tensor_reduce(blk_max[:, m + 2 * h:m + 2 * h + 2, 1:4],
                                      ps[:, 2 * st:2 * st + 2, 0:SPAN].rearrange("p a (c k) -> p a c k", k=P),
                                      AX_X, ALU.max, negate=True).then_inc(s_max, 1)
                dve.wait_ge(s_max, (b * GROUPS + g) * 2 + 2)
                dve.tensor_reduce(neg_max[:, :, m:m + 4].rearrange("p i r -> p r i"),
                                  blk_max[:, m:m + 4, :].rearrange("p r (i two) -> p r i two", two=2),
                                  AX_X, ALU.min).then_inc(s_row, 1)

            def scale(b, g):
                o = ps[:, B_O, SEQ:2 * SEQ].rearrange("p (i r d) -> p i r d", i=HALVES, d=SLOT)
                dve.wait_ge(s_ot, b * GROUPS + g + 1)
                dve.reciprocal(o_inv[:], o[:, :, :, VD]).then_inc(s_inv, 1)
                dve.wait_ge(s_inv, (b * GROUPS + g) * 2 + 1)
                odd = o_inv[:].rearrange("p i (n two) -> p i n two", two=2)[:, :, :, 1]
                dve.tensor_scalar(odd, odd, neg_lam[:], None, ALU.mult).then_inc(s_inv, 1)
                if g >= 2:
                    dve.wait_ge(s_dif, b * GROUPS + g - 1)
                dve.wait_ge(s_inv, (b * GROUPS + g) * 2 + 2)
                dve.tensor_tensor(o_sc[:, g % 2], o[:, :, :, 0:VD],
                                  o_inv[:].unsqueeze(3).to_broadcast([P, HALVES, 4, VD]), ALU.mult)\
                    .then_inc(s_scaled, 1)

            def sum_squares(b, g):
                dve.wait_ge(s_sq, b * GROUPS + g + 1)
                o = o_ms[:].rearrange("p (t n) -> p t n", n=HEADS)
                dve.tensor_reduce(rows_of(o, b, g, slice(2 * (g % GROUPS), 2 * (g % GROUPS) + 2)),
                                  o_sq[:, g % 2], AX_X, ALU.add).then_inc(s_ms, 1)

            def attention(b, u):
                if u < ALL_GROUPS:
                    row_max(b, u)
                if 0 <= u - LAG_SUM < ALL_GROUPS:
                    sum_squares(b, u - LAG_SUM)
                if 0 <= u - LAG_PV < ALL_GROUPS:
                    scale(b, u - LAG_PV)

            def normalise():
                dve.wait_ge(s_ms, ALL_GROUPS)
                dve.tensor_scalar(o_me[:], o_ms[:], 1.0 / VD, RMS_EPS, ALU.mult, ALU.add).then_inc(s_mean, 1)
                dve.wait_ge(s_root, 1)
                chain.step(dve.reciprocal(o_rs[:], o_me[:]))
                for j in range(TILES):
                    o = attn[:, j, :].rearrange("p (n d) -> p n d", d=VD)
                    dve.tensor_tensor(o, o, o_rs[:, j * HEADS:(j + 1) * HEADS].unsqueeze(2)
                                      .to_broadcast([P, HEADS, VD]), ALU.mult).then_inc(s_attn, 1)

            dve.memset(tile_expert[:, 0:TILES], SHARED).then_inc(s_dve, 1)
            chain.n += 1
            dve.wait_ge(s_const, N_CONST)
            dve.wait_ge(s_small, 16 * N_SMALL)
            dve.tensor_copy(tables[:].rearrange("p n m -> p (n m)"), work[:, 0, :]).then_inc(s_tables, 1)
            dve.tensor_copy(ident_r[:], ident[:]).then_inc(s_tables, 1)
            layernorm(0, loaded)
            plan(0)
            experts(0)
            dve.wait_ge(s_late, 16 * N_LATE)
            pairs = lam_in[:].rearrange("p (n two) d -> p n two d", two=2)
            chain.step(dve.tensor_tensor(lam_pr[:], pairs[:, :, 0, :], pairs[:, :, 1, :], ALU.mult))
            dve.tensor_reduce(lam_s[:], lam_pr[:], AX_X, ALU.add).then_inc(s_lam, 1)
            dve.wait_ge(s_watt, 16 * 4)
            dve.tensor_scalar(w_o[:], w_o[:], g_col[:], 1.0 - LAMBDA_INIT, ALU.mult, ALU.mult)\
                .then_inc(s_wo, 1)
            dve.wait_ge(s_lame, 1)
            chain.step(dve.scalar_tensor_tensor(neg_lam[:], lam_e[:, 1:2], -LAMBDA_INIT, lam_e[:, 0:1],
                                                ALU.add, ALU.subtract))
            layernorm(1, add_routed(0))
            rotary()
            attention_steps(dve, attention)
            normalise()
            layernorm(2, add_projected)
            plan(1)
            experts(1)
            for j in range(TILES):
                add_routed(1)(j)

        @block.scalar
        def _(act):
            act.wait_ge(s_x[TURNS - 1], 16)
            halves = ((sh_gate, 0), (sh_up, INNER))
            for w, at in halves:
                act.dma_start(w_gu[:, SHARED, :, at:at + INNER], w.rearrange("(c p) f -> p c f", p=P))\
                    .then_inc(s_wsh, 16)
            act.dma_start(w_dn[:, SHARED], sh_down.rearrange("(c p) d -> p c d", p=P)).then_inc(s_wsh, 16)
            for e in range(EXPERTS):
                act.dma_start(w_gu[:, e], gate_up[e].rearrange("(c p) f -> p c f", p=P))\
                    .then_inc(s_wex, 16)
                act.dma_start(w_dn[:, e], down[e].rearrange("(c p) d -> p c d", p=P))\
                    .then_inc(s_wex, 16)
            for w, at in ((wq, 0), (wk, DIM), (wv, DIM + KV_HEADS * VD)):
                act.dma_start(w_qkv[:, :, at:at + w.shape[1]], w.rearrange("(c p) n -> p c n", p=P))\
                    .then_inc(s_watt, 16)
            act.dma_start(w_o[:], wo.rearrange("(c p) n -> p c n", p=P)).then_inc(s_watt, 16)
            act.dma_start(rope[:], rope_in.rearrange("(i p) a d -> p i a d", p=P)).then_inc(s_late, 16)
            for n, v in enumerate((lam_q1, lam_k1, lam_q2, lam_k2)):
                act.dma_start(lam_in[:, n, :], v.rearrange("(a d) -> a d", a=1).to_broadcast([P, HD]))\
                    .then_inc(s_late, 16)
            for h in range(P // VD):
                act.dma_start(g_col[h * VD:(h + 1) * VD, :], g.rearrange("(d a) -> d a", a=1))\
                    .then_inc(s_late, 16)

            def turned(n):
                for f in range(TURNS):
                    act.wait_ge(s_turn, n * TURNS + f + 1)
                    act.activation(xn_t[:, 2 * f:2 * f + 2].rearrange("p a c t -> p (a c t)"),
                                   ps[:, B_TURN[f % 2], :], ACT.Copy).then_inc(s_turned, 1)

            def experts(k):
                s = ffn[k]

                def tile(i):
                    act.wait_ge(s["gate_up_done"], i + 1)
                    act.wait_ge(s["hidden_ready"], i)
                    act.activation(act_g, ps[:, B_GATE, :], ACT.Silu).then_inc(s["silu_done"], 1)
                    act.wait_ge(s["hidden_turned"], i + 1)
                    act.wait_ge(s["y_done"], i)
                    act.activation(hid_t.rearrange("p c t -> p (c t)"), ps[:, B_HT, :], ACT.Copy)\
                        .then_inc(s["hidden_t_ready"], 1)

                act.wait_ge(s["top_ready"], 1)
                act.activation(score[:], top[:], ACT.Sigmoid).then_inc(s["score_ready"], 1)
                tile(0)
                with act.Fori(1, TILES) as i:
                    tile(i)
                act.wait_ge(s["plan_ready"], 2)
                n = tile_count(act)
                with act.Fori(TILES, n) as i:
                    tile(i)

            def copy_v():
                for j in range(TILES):
                    act.wait_ge(s_clamp, j + 1)
                    act.activation(v_all[:, j, :],
                                   ps[:, j % 2, SPAN:N_QKV],
                                   ACT.Copy).then_inc(s_vall, 1)

            def copy_qk(b, g):
                act.wait_ge(s_fill, b * GROUPS + g + 1)
                act.activation(qk_t[:, g % RING_T].rearrange("p a t -> p (a t)"), ps[:, B_MISC, :], ACT.Copy)\
                    .then_inc(s_filc, 1)

            def copy_qm(b, g):
                act.wait_ge(s_qm, b * GROUPS + g + 1)
                act.activation(qm_t[:, g % 2, :], ps[:, B_MISC, 0:SEQ], ACT.Copy).then_inc(s_qmc, 1)

            def copy_o(b, g):
                act.wait_ge(s_pv, b * GROUPS + g + 1)
                act.activation(o_t, ps[:, B_O, 0:SEQ], ACT.Copy).then_inc(s_oc, 1)

            def exponentials(b, g):
                for h in range(2):
                    st = SET_OF["B", h]
                    act.wait_ge(s_bscore, (b * GROUPS + g) * 2 + h + 1)
                    act.activation(probs[:, (2 * g + h) % 4], ps[:, 2 * st:2 * st + 2, 0:SPAN],
                                   ACT.Exp, scale=HD ** -0.5).then_inc(s_exp, 1)

            def attention(b, u):
                if 0 <= u - LAG_B < ALL_GROUPS:
                    copy_qm(b, u - LAG_B)
                if 0 <= u - LAG_PV < ALL_GROUPS:
                    copy_o(b, u - LAG_PV)
                if 0 <= u - LAG_B < ALL_GROUPS:
                    exponentials(b, u - LAG_B)
                if u + 2 < ALL_GROUPS:
                    copy_qk(b, u + 2)

            turned(0)
            experts(0)
            act.wait_ge(s_lam, 1)
            act.activation(lam_e[:], lam_s[:], ACT.Exp).then_inc(s_lame, 1)
            turned(1)
            copy_v()
            copy_qk(0, 0)
            copy_qk(0, 1)
            attention_steps(act, attention)
            act.wait_ge(s_mean, 1)
            act.activation(o_me[:], o_me[:], ACT.Sqrt).then_inc(s_root, 1)
            turned(2)
            turned(3)
            experts(1)

        @block.tensor
        def _(pe):
            def turn(n, src, ready):
                for f in range(TURNS):
                    ready(f)
                    if n * TURNS + f >= 2:
                        pe.wait_ge(s_turned, n * TURNS + f - 1)
                    for m in range(2 * KC):
                        j, c = 2 * f + m // KC, m % KC
                        ins = pe.transpose(ps[:, B_TURN[f % 2], m * P:(m + 1) * P],
                                           src[:, j, c * P:(c + 1) * P], ident[:])
                    ins.then_inc(s_turn, 1)

            def ln_ready(n):
                return lambda f: pe.wait_ge(s_xn, n * TILES + 2 * f + 2)

            def route(k):
                s = ffn[k]
                n = (0, 3)[k]
                pe.wait_ge(s_turned, (n + 1) * TURNS)
                for j in range(TILES):
                    for c in range(KC):
                        ins = pe.matmul(ps[:, B_LOGIT, j * EXPERTS:(j + 1) * EXPERTS], xn_t[:, j, c, :],
                                        w_rt[:, c, :], start=(c == 0), stop=(c == KC - 1))
                ins.then_inc(s["logits_done"], 1)
                pe.wait_ge(s["onehot_ready"], 1)
                for d in range(TILES):
                    pe.matmul(ps[:, B_RANK, d * EXPERTS:TILES * EXPERTS], before if d == 0 else ones_b[:],
                              onehot_b[:, 0:TILES - d].rearrange("p t e -> p (t e)"),
                              start=(d == 0), stop=(d == TILES - 1), skip_group_check=True)
                for j in range(TILES):
                    ins = pe.matmul(ps[:, B_COUNT, 0:EXPERTS], ones_b[:], onehot_b[:, j, :],
                                    start=(j == 0), stop=(j == TILES - 1))
                ins.then_inc(s["ranks_done"], 1)

            def experts(k):
                s = ffn[k]

                def turn_x(i):
                    pe.wait_ge(s["tile_loaded"], (i - (TILES - 1)) * 16)
                    pe.wait_ge(s["tile_t_ready"], i)
                    for c in range(KC):
                        ins = pe.transpose(ps[:, B_XT, c * P:(c + 1) * P], x_tile[:, c * P:(c + 1) * P],
                                           ident[:])
                    ins.then_inc(s["tile_turned"], 1)

                def gate_up_of(i, w):
                    pe.wait_ge(s["tile_t_ready"], i + 1)
                    pe.wait_ge(s["hidden_ready"], i)
                    for h, bank in enumerate((B_GATE, B_UP)):
                        for c in range(KC):
                            ins = pe.matmul(ps[:, bank, :], x_t[:, c, :], w(c, h),
                                            start=(c == 0), stop=(c == KC - 1))
                    ins.then_inc(s["gate_up_done"], 1)

                def turn_hidden(i):
                    pe.wait_ge(s["hidden_ready"], i + 1)
                    pe.wait_ge(s["hidden_t_ready"], i)
                    for c in range(FC):
                        ins = pe.transpose(ps[:, B_HT, c * P:(c + 1) * P], hid[:, c * P:(c + 1) * P],
                                           ident[:])
                    ins.then_inc(s["hidden_turned"], 1)

                def down_of(i, w):
                    pe.wait_ge(s["hidden_t_ready"], i + 1)
                    pe.wait_ge(s["y_ready"], i)
                    for c in range(FC):
                        ins = pe.matmul(ps[:, B_Y, 0:DIM], hid_t[:, c, :], w(c),
                                        start=(c == 0), stop=(c == FC - 1))
                    ins.then_inc(s["y_done"], 1)

                def shared_gu(c, h):
                    return w_gu[:, SHARED, c, h * INNER:(h + 1) * INNER]

                def shared_dn(c):
                    return w_dn[:, SHARED, c, :]

                def expert_of(i):
                    return pe.value_load(tile_expert[0:1, bass.ds(i, 1)], min_val=0, max_val=EXPERTS)

                def gu(e):
                    return lambda c, h: w_gu[:, bass.ds(e, 1), c, h * INNER:(h + 1) * INNER]\
                        .rearrange("p a n -> p (a n)")

                def dn(e):
                    return lambda c: w_dn[:, bass.ds(e, 1), c, :].rearrange("p a n -> p (a n)")

                if k == 0:
                    pe.wait_ge(s_wsh, 16 * 3)
                gate_up_of(0, shared_gu)
                turn_hidden(0)

                def shared_tile(i, last=False):
                    gate_up_of(i, shared_gu)
                    down_of(i - 1, shared_dn)
                    if last:
                        turn_x(TILES)
                    turn_hidden(i)

                shared_tile(1)
                with pe.Fori(2, TILES - 1) as i:
                    shared_tile(i)
                shared_tile(TILES - 1, last=True)
                pe.wait_ge(s["plan_ready"], 2)
                if k == 0:
                    pe.wait_ge(s_wex, 16 * 2 * EXPERTS)
                n = tile_count(pe)
                with pe.Fori(TILES, n) as i:
                    e, e_before = expert_of(i), expert_of(i - 1)
                    gate_up_of(i, gu(e))
                    turn_x(i + 1)
                    down_of(i - 1, dn(e_before))
                    turn_hidden(i)
                last = tile_count(pe, 1)
                down_of(last, dn(expert_of(last)))

            def qkv():
                pe.wait_ge(s_watt, 16 * 4)
                for j in range(TILES):
                    pe.wait_ge(s_turned, TURNS + j // 2 + 1)
                    if j >= 2:
                        pe.wait_ge(s_vall, j - 1)
                    for c in range(KC):
                        ins = pe.matmul(ps[:, j % 2, :], xn_t[:, j, c, :], w_qkv[:, c, :],
                                        start=(c == 0), stop=(c == KC - 1))
                    ins.then_inc(s_qkv, 1)

            def scores(b, kind, g, h):
                st = SET_OF[kind, h]
                mask = mask_ts if kind == "A" else mask_st
                for m in range(2):
                    bank = ps[:, 2 * st + m, :]
                    pe.matmul(bank.rearrange("p (a c) -> p a c", a=2)[:, :, 0:P], ident_b,
                              mask.unsqueeze(1).to_broadcast([P, 2, P]), start=True, stop=False,
                              skip_group_check=True)
                for part in range(2):
                    for m in range(2):
                        r = SLOT * (2 * h + m)
                        bank = ps[:, 2 * st + m, :]
                        if kind == "A":
                            rows = slice(r, r + ROWS_A)
                            w = qk_t[rows, g % RING_T, 0, part * P:(part + 1) * P]
                            x = qk_t[rows, g % RING_T, 1, 0:(part + 1) * P]
                            o = bank[:, 0:P] if part == 0 else bank[:, P:SPAN]
                        else:
                            rows = slice(r, r + ROWS_B)
                            w = qk_t[rows, g % RING_T, 1, part * P:(part + 1) * P]
                            x = qm_t[rows, g % 2, part * P:SEQ]
                            o = bank[:, 0:SEQ] if part == 0 else bank[:, SEQ:SPAN]
                        ins = pe.matmul(o, w, x, start=False, stop=True, skip_group_check=True)
                ins.then_inc(s_ascore if kind == "A" else s_bscore, 1)

            def turn_pads(g, keys):
                for i in range(HALVES):
                    pad = k_pad[:, g % RING_T, i] if keys else q_pad[:, g % RING, i]
                    w = pad.rearrange("p n s -> p (n s)")
                    at = (HALVES * keys + i) * P
                    ins = pe.matmul(ps[:, B_MISC, at:at + P], w, ident_r[:], start=True, stop=True,
                                    skip_group_check=True)
                return ins

            def turn_qk(b, g):
                pe.wait_ge(s_pad, (b * GROUPS + g + 1) * 2)
                if g >= 1:
                    pe.wait_ge(s_filc, b * GROUPS + g)
                turn_pads(g, 0)
                turn_pads(g, 1).then_inc(s_fill, 1)

            def p_v(b, g):
                pe.wait_ge(s_exp, (b * GROUPS + g) * 2 + 2)
                if g >= 1:
                    pe.wait_ge(s_scaled, b * GROUPS + g)
                for i in range(HALVES):
                    for r in range(4):
                        pr = probs[:, (2 * g + r // 2) % 4, r % 2, :]
                        ins = pe.matmul(ps[SLOT * r:SLOT * (r + 1), B_O, i * P:SEQ], v_pad[:, g % RING, i, :],
                                        pr[:, 0:SEQ] if i == 0 else pr[:, SEQ:SPAN],
                                        start=(i == 0), stop=(i == 1), skip_group_check=True)
                ins.then_inc(s_pv, 1)

            def turn_o(b, g):
                pe.wait_ge(s_oc, b * GROUPS + g + 1)
                for i in range(HALVES):
                    ins = pe.transpose(ps[:, B_O, SEQ + i * P:SEQ + (i + 1) * P], o_t[:, i * P:(i + 1) * P],
                                       ident[:])
                ins.then_inc(s_ot, 1)

            def attention(b, u):
                g_b, g_pv = u - LAG_B, u - LAG_PV
                with_b, with_pv = 0 <= g_b < ALL_GROUPS, 0 <= g_pv < ALL_GROUPS
                if u < ALL_GROUPS:
                    pe.wait_ge(s_filc, b * GROUPS + u + 1)
                    if g_b >= 1:
                        pe.wait_ge(s_exp, (b * GROUPS + g_b) * 2 - 1)
                    elif u >= 1:
                        pe.wait_ge(s_max, 2 * u - 1)
                    scores(b, "A", u, 0)
                    if u >= 1:
                        pe.wait_ge(s_max, (b * GROUPS + u) * 2)
                    scores(b, "A", u, 1)
                if with_b:
                    pe.wait_ge(s_neg, b * GROUPS + g_b + 1)
                    if u + 1 < ALL_GROUPS:
                        pe.wait_ge(s_filc, b * GROUPS + u + 2)
                    turn_pads(g_b, 0).then_inc(s_qm, 1)
                if with_pv:
                    p_v(b, g_pv)
                if with_b:
                    pe.wait_ge(s_qmc, b * GROUPS + g_b + 1)
                    if u < ALL_GROUPS:
                        pe.wait_ge(s_max, (b * GROUPS + u) * 2 + 1)
                    else:
                        pe.wait_ge(s_exp, (b * GROUPS + g_b) * 2 - 1)
                    scores(b, "B", g_b, 0)
                if with_pv:
                    turn_o(b, g_pv)
                if with_b:
                    if g_b >= 1:
                        pe.wait_ge(s_exp, (b * GROUPS + g_b) * 2)
                    scores(b, "B", g_b, 1)
                if u + 2 < ALL_GROUPS:
                    turn_qk(b, u + 2)

            def full_clock():
                pe.wait_ge(s_exp, (FIRST - LAG_B) * 2 - 1)
                for _ in range(WARM_UP):
                    pe.matmul(ps[:, 2 * SET_OF["A", 0], :], ident[:], w_gu[:, SHARED, 0, 0:INNER],
                              start=True, stop=True)

            def project():
                pe.wait_ge(s_wo, 1)
                for j in range(TILES):
                    pe.wait_ge(s_turned, 2 * TURNS + j // 2 + 1)
                    if j >= 2:
                        pe.wait_ge(s_res, TILES + j - 1)
                    for c in range(KC):
                        ins = pe.matmul(ps[:, j % 2, 0:DIM], xn_t[:, j, c, :], w_o[:, c, :],
                                        start=(c == 0), stop=(c == KC - 1))
                    ins.then_inc(s_proj, 1)

            pe.wait_ge(s_small, 16 * N_SMALL)
            pe.wait_ge(s_const, N_CONST)
            pe.wait_ge(s_tables, 2)
            turn(0, xn, ln_ready(0))
            route(0)
            experts(0)
            turn(1, xn, ln_ready(1))
            qkv()
            turn_qk(0, 0)
            turn_qk(0, 1)
            attention_steps(pe, attention, full_clock)
            turn(2, attn, lambda f: pe.wait_ge(s_attn, 2 * f + 2))
            project()
            turn(3, xn, ln_ready(2))
            route(1)
            experts(1)


_INS = ["L0_attn_x", "L0_attn_Wq", "L0_attn_Wk", "L0_attn_Wv", "L0_attn_Wo", "L0_attn_lam_q1",
        "L0_attn_lam_k1", "L0_attn_lam_q2", "L0_attn_lam_k2", "L0_attn_g", "L0_ffn_router_w",
        "L0_ffn_gate_up_proj", "L0_ffn_down_proj", "L0_ffn_shared_gate_w", "L0_ffn_shared_up_w",
        "L0_ffn_shared_down_w"]


def _constants():
    import numpy as np
    at = np.arange(P)
    hidden = np.float32(-3e38)
    tables = np.stack([np.eye(P), np.where(at[None, :] > at[:, None], hidden, 0.0),
                       np.where(at[:, None] > at[None, :], hidden, 0.0),
                       at[:, None] < at[None, :]], axis=1).astype(np.float32)
    freq = (1.0 / 10000.0 ** (np.arange(0, HD, 2, dtype=np.float32) / HD)).astype(np.float32)
    angle = np.arange(SEQ, dtype=np.float32)[:, None] * freq[None, :]
    cos, sin = np.cos(angle), np.sin(angle)
    rope = np.stack([np.concatenate([cos, cos], 1), np.concatenate([sin, -sin], 1)], axis=1)
    return {"ident": np.eye(P, dtype=np.float32), "tables": tables, "rope": rope.astype(np.float32)}


def kernel(**inputs):
    import numpy as _np
    import concourse.bacc as _bacc
    from concourse import mybir as _mybir
    from concourse.bass_utils import run_bass_kernel_spmd as _run

    nc = _bacc.Bacc("TRN2", target_bir_lowering=False, num_devices=1)
    given = {name: _np.asarray(inputs[name]) for name in _INS}
    given["L0_ffn_router_w"] = given["L0_ffn_router_w"].T
    given.update(_constants())
    arrays, args = {}, []
    for name, a in given.items():
        a = _np.ascontiguousarray(a)
        arrays[f"in_{name}_dram"] = a
        args.append(nc.dram_tensor(f"in_{name}_dram", a.shape, _mybir.dt.from_np(a.dtype), kind="ExternalInput").ap())
    args.append(nc.dram_tensor("out_0_dram", (BATCH, SEQ, DIM), F32, kind="ExternalOutput").ap())
    bass_macaron(nc, *args)
    r = _run(nc, [arrays], core_ids=[0])
    return r.results[0]["out_0_dram"]
```
